# Optimizing a Trainium2 kernel written in Bass

```python
import numpy as np
import jax
import jax.numpy as jnp

def _softmax(x, axis=-1):
    return jax.nn.softmax(x, axis=axis)
def _gelu(x):
    return jax.nn.gelu(x, approximate=True)
def _silu(x):
    return jax.nn.silu(x)
def _sigmoid(x):
    return jax.nn.sigmoid(x)
def _layernorm(x, axis=-1, eps=1e-5):
    m = jnp.mean(x, axis=axis, keepdims=True)
    v = jnp.var(x, axis=axis, keepdims=True)
    return (x - m) / jnp.sqrt(v + eps)
def _scatter_add(tgt, idx, src, axis=0):
    return tgt.at[idx].add(src)
def _segment_sum(src, seg, n):
    return jax.ops.segment_sum(src, seg, n)

kernel_name = 'mk_conv_preact_d2_conv_nchw64_20f656'

def setup_inputs(seed: int = 0):
    np.random.seed(seed)
    _w = jnp.asarray
    def _rec_inputs():
        import jax
        import jax.numpy as jnp
        _gk = jax.random.key(seed)
        x = -0.000125 + 0.9999 * jax.random.normal(jax.random.fold_in(_gk, 1), (8, 64, 256, 256), jnp.float32)
        return x
    x = _rec_inputs()
    def _L0_conv_setup():
        import jax, jax.numpy as jnp
        import numpy as np
        silu = jax.nn.silu
        EPS = 1e-05
        GROUPS = 8

        def conv2d(x, w, b=None, pad=0, groups=1):
            out = jax.lax.conv_general_dilated(x, w, window_strides=(1, 1), padding=[(pad, pad), (pad, pad)], dimension_numbers=('NCHW', 'OIHW', 'NCHW'), feature_group_count=groups)
            if b is not None:
                out = out + b[None, :, None, None]
            return out

        def group_norm(x, gamma, beta, groups=GROUPS, eps=EPS):
            B, C, H, W = x.shape
            xg = x.reshape(B, groups, C // groups, H, W)
            mu = xg.mean(axis=(2, 3, 4), keepdims=True)
            var = xg.var(axis=(2, 3, 4), keepdims=True)
            xg = (xg - mu) * jax.lax.rsqrt(var + eps)
            x = xg.reshape(B, C, H, W)
            return x * gamma[None, :, None, None] + beta[None, :, None, None]
        key = jax.random.key(seed)
        ks = jax.random.split(key, 16)
        Ci, Co = (64, 64)
        B, H, W = (8, 256, 256)
        s = 0.1
        return {'x': jax.random.normal(ks[0], (B, Ci, H, W), dtype=jnp.float32), 'conv1_w': jax.random.normal(ks[1], (Co, Ci, 1, 1), jnp.float32) * s, 'conv1_b': jnp.zeros((Co,), jnp.float32), 'dw1_w': jax.random.normal(ks[2], (Co, 1, 1, 1), jnp.float32) * s, 'dw1_b': jnp.zeros((Co,), jnp.float32), 'dw2_w': jax.random.normal(ks[3], (Co, 1, 3, 3), jnp.float32) * s, 'dw2_b': jnp.zeros((Co,), jnp.float32), 'dw3_w': jax.random.normal(ks[4], (Co, 1, 5, 5), jnp.float32) * s, 'dw3_b': jnp.zeros((Co,), jnp.float32), 'pw_w': jax.random.normal(ks[5], (Ci, 3 * Co, 1, 1), jnp.float32) * s, 'pw_b': jnp.zeros((Ci,), jnp.float32), 'ca_w1': jax.random.normal(ks[6], (Ci // 8, Ci, 1, 1), jnp.float32) * s, 'ca_w2': jax.random.normal(ks[7], (Ci, Ci // 8, 1, 1), jnp.float32) * s, 'sa_w': jax.random.normal(ks[8], (1, 2, 7, 7), jnp.float32) * s, 'sa_b': jnp.zeros((1,), jnp.float32), 'gn_g': jnp.ones((Ci,), jnp.float32), 'gn_b': jnp.zeros((Ci,), jnp.float32)}
    _L0_conv_all = _L0_conv_setup()
    _L0_conv_in = {k: v for k, v in _L0_conv_all.items() if k in ('conv1_w', 'conv1_b', 'dw1_w', 'dw1_b', 'dw2_w', 'dw2_b', 'dw3_w', 'dw3_b', 'pw_w', 'pw_b', 'ca_w1', 'ca_w2', 'sa_w', 'sa_b', 'gn_g', 'gn_b', )}
    del _L0_conv_all

    def _L1_conv_setup():
        import jax, jax.numpy as jnp
        import numpy as np
        from jax import lax
        DIM = 64
        E = int(DIM * 1.2)
        E4 = E * 4
        P = 8
        B, H, W = (2, 256, 256)
        THR = 1e-10

        def _replace_denormals(z, thr=THR):
            r, i = (z.real, z.imag)
            r = jnp.where((r < thr) & (r > -thr), thr, r)
            i = jnp.where((i < thr) & (i > -thr), thr, i)
            return lax.complex(r, i)

        def _patch(t):
            b, c, h, w = t.shape
            return t.reshape(b, c, h // P, P, w // P, P).transpose(0, 1, 2, 4, 3, 5)

        def _unpatch(t):
            b, c, h, w, p1, p2 = t.shape
            return t.transpose(0, 1, 2, 4, 3, 5).reshape(b, c, h * p1, w * p2)

        def _layernorm(t, w, b):
            mu = jnp.mean(t, axis=1, keepdims=True)
            var = jnp.mean((t - mu) ** 2, axis=1, keepdims=True)
            return (t - mu) / jnp.sqrt(var + 1e-05) * w[None, :, None, None] + b[None, :, None, None]
        key = jax.random.key(seed)
        ks = jax.random.split(key, 5)
        x = jax.random.normal(ks[0], (B, DIM, H, W), dtype=jnp.float32)
        w_hidden = jax.random.normal(ks[1], (E4, DIM), dtype=jnp.float32) * 0.05
        w_dw = jax.random.normal(ks[2], (E4, 1, 3, 3), dtype=jnp.float32) * 0.2
        w_proj = jax.random.normal(ks[3], (DIM, 3 * E), dtype=jnp.float32) * 0.05
        fft_param = jnp.ones((E, 1, 1, P, P // 2 + 1), dtype=jnp.float32)
        ln1_w = jnp.ones((E,), jnp.float32)
        ln1_b = jnp.zeros((E,), jnp.float32)
        ln2_w = jnp.ones((E,), jnp.float32)
        ln2_b = jnp.zeros((E,), jnp.float32)
        ln3_w = jnp.ones((E,), jnp.float32)
        ln3_b = jnp.zeros((E,), jnp.float32)
        return dict(x=x, w_hidden=w_hidden, w_dw=w_dw, w_proj=w_proj, fft_param=fft_param, ln1_w=ln1_w, ln1_b=ln1_b, ln2_w=ln2_w, ln2_b=ln2_b, ln3_w=ln3_w, ln3_b=ln3_b)
    _L1_conv_all = _L1_conv_setup()
    _L1_conv_in = {k: v for k, v in _L1_conv_all.items() if k in ('w_hidden', 'w_dw', 'w_proj', 'fft_param', 'ln1_w', 'ln1_b', 'ln2_w', 'ln2_b', 'ln3_w', 'ln3_b', )}
    del _L1_conv_all

    return {
        "x": x,
        "L0_conv_conv1_w": _L0_conv_in["conv1_w"],
        "L0_conv_conv1_b": _L0_conv_in["conv1_b"],
        "L0_conv_dw1_w": _L0_conv_in["dw1_w"],
        "L0_conv_dw1_b": _L0_conv_in["dw1_b"],
        "L0_conv_dw2_w": _L0_conv_in["dw2_w"],
        "L0_conv_dw2_b": _L0_conv_in["dw2_b"],
        "L0_conv_dw3_w": _L0_conv_in["dw3_w"],
        "L0_conv_dw3_b": _L0_conv_in["dw3_b"],
        "L0_conv_pw_w": _L0_conv_in["pw_w"],
        "L0_conv_pw_b": _L0_conv_in["pw_b"],
        "L0_conv_ca_w1": _L0_conv_in["ca_w1"],
        "L0_conv_ca_w2": _L0_conv_in["ca_w2"],
        "L0_conv_sa_w": _L0_conv_in["sa_w"],
        "L0_conv_sa_b": _L0_conv_in["sa_b"],
        "L0_conv_gn_g": _L0_conv_in["gn_g"],
        "L0_conv_gn_b": _L0_conv_in["gn_b"],
        "L1_conv_w_hidden": _L1_conv_in["w_hidden"],
        "L1_conv_w_dw": _L1_conv_in["w_dw"],
        "L1_conv_w_proj": _L1_conv_in["w_proj"],
        "L1_conv_fft_param": _L1_conv_in["fft_param"],
        "L1_conv_ln1_w": _L1_conv_in["ln1_w"],
        "L1_conv_ln1_b": _L1_conv_in["ln1_b"],
        "L1_conv_ln2_w": _L1_conv_in["ln2_w"],
        "L1_conv_ln2_b": _L1_conv_in["ln2_b"],
        "L1_conv_ln3_w": _L1_conv_in["ln3_w"],
        "L1_conv_ln3_b": _L1_conv_in["ln3_b"],
    }

def reference(x, L0_conv_conv1_w, L0_conv_conv1_b, L0_conv_dw1_w, L0_conv_dw1_b, L0_conv_dw2_w, L0_conv_dw2_b, L0_conv_dw3_w, L0_conv_dw3_b, L0_conv_pw_w, L0_conv_pw_b, L0_conv_ca_w1, L0_conv_ca_w2, L0_conv_sa_w, L0_conv_sa_b, L0_conv_gn_g, L0_conv_gn_b, L1_conv_w_hidden, L1_conv_w_dw, L1_conv_w_proj, L1_conv_fft_param, L1_conv_ln1_w, L1_conv_ln1_b, L1_conv_ln2_w, L1_conv_ln2_b, L1_conv_ln3_w, L1_conv_ln3_b):
    import jax
    import jax.numpy as jnp
    def _L0_conv_ref(x, conv1_w, conv1_b, dw1_w, dw1_b, dw2_w, dw2_b, dw3_w, dw3_b, pw_w, pw_b, ca_w1, ca_w2, sa_w, sa_b, gn_g, gn_b):
        import jax, jax.numpy as jnp
        import numpy as np
        silu = jax.nn.silu
        EPS = 1e-05
        GROUPS = 8

        def conv2d(x, w, b=None, pad=0, groups=1):
            out = jax.lax.conv_general_dilated(x, w, window_strides=(1, 1), padding=[(pad, pad), (pad, pad)], dimension_numbers=('NCHW', 'OIHW', 'NCHW'), feature_group_count=groups)
            if b is not None:
                out = out + b[None, :, None, None]
            return out

        def group_norm(x, gamma, beta, groups=GROUPS, eps=EPS):
            B, C, H, W = x.shape
            xg = x.reshape(B, groups, C // groups, H, W)
            mu = xg.mean(axis=(2, 3, 4), keepdims=True)
            var = xg.var(axis=(2, 3, 4), keepdims=True)
            xg = (xg - mu) * jax.lax.rsqrt(var + eps)
            x = xg.reshape(B, C, H, W)
            return x * gamma[None, :, None, None] + beta[None, :, None, None]
        Co = conv1_w.shape[0]
        x_init = x
        h = silu(conv2d(x, conv1_w, conv1_b))
        h1 = conv2d(h, dw1_w, dw1_b, pad=0, groups=Co)
        h2 = conv2d(h, dw2_w, dw2_b, pad=1, groups=Co)
        h3 = conv2d(h, dw3_w, dw3_b, pad=2, groups=Co)
        h = jnp.concatenate([h1, h2, h3], axis=1)
        h = silu(conv2d(h, pw_w, pw_b)) + x_init
        h = silu(h)
        avg_p = h.mean(axis=(2, 3), keepdims=True)
        max_p = h.max(axis=(2, 3), keepdims=True)
        mlp = lambda p: conv2d(jax.nn.relu(conv2d(p, ca_w1)), ca_w2)
        ca = silu(mlp(avg_p) + mlp(max_p))
        out = ca * h
        sp = jnp.concatenate([out.mean(axis=1, keepdims=True), out.max(axis=1, keepdims=True)], axis=1)
        sa = silu(conv2d(sp, sa_w, sa_b, pad=3))
        out = sa * out
        return silu(group_norm(out, gn_g, gn_b))

    def _L1_conv_ref(x, w_hidden, w_dw, w_proj, fft_param, ln1_w, ln1_b, ln2_w, ln2_b, ln3_w, ln3_b):
        import jax, jax.numpy as jnp
        import numpy as np
        from jax import lax
        DIM = 64
        E = int(DIM * 1.2)
        E4 = E * 4
        P = 8
        B, H, W = (2, 256, 256)
        THR = 1e-10

        def _replace_denormals(z, thr=THR):
            r, i = (z.real, z.imag)
            r = jnp.where((r < thr) & (r > -thr), thr, r)
            i = jnp.where((i < thr) & (i > -thr), thr, i)
            return lax.complex(r, i)

        def _patch(t):
            b, c, h, w = t.shape
            return t.reshape(b, c, h // P, P, w // P, P).transpose(0, 1, 2, 4, 3, 5)

        def _unpatch(t):
            b, c, h, w, p1, p2 = t.shape
            return t.transpose(0, 1, 2, 4, 3, 5).reshape(b, c, h * p1, w * p2)

        def _layernorm(t, w, b):
            mu = jnp.mean(t, axis=1, keepdims=True)
            var = jnp.mean((t - mu) ** 2, axis=1, keepdims=True)
            return (t - mu) / jnp.sqrt(var + 1e-05) * w[None, :, None, None] + b[None, :, None, None]
        hidden = jnp.einsum('bchw,oc->bohw', x, w_hidden)
        hdw = lax.conv_general_dilated(hidden, w_dw, window_strides=(1, 1), padding='SAME', dimension_numbers=('NCHW', 'OIHW', 'NCHW'), feature_group_count=E4)
        q, k, v, v_value = jnp.split(hdw, 4, axis=1)
        qf = jnp.fft.rfft2(_patch(q))
        kf = jnp.fft.rfft2(_patch(k))
        vf = jnp.fft.rfft2(_patch(v)) * fft_param
        vf = _replace_denormals(vf)
        qk = _replace_denormals(qf * kf)
        qka = jnp.abs(qk)
        v_a = jnp.abs(vf)
        v_p = jnp.arctan2(vf.imag, vf.real)
        qf = _replace_denormals(qf)
        kf = _replace_denormals(kf)
        qkp = jnp.arctan2(qf.imag, qf.real) - jnp.arctan2(kf.imag, kf.real)
        out1 = jnp.fft.irfft2(lax.complex(v_a * jnp.cos(qkp), v_a * jnp.sin(qkp)), s=(P, P))
        out2 = jnp.fft.irfft2(lax.complex(qka * jnp.cos(v_p), qka * jnp.sin(v_p)), s=(P, P))
        out3 = jnp.fft.irfft2(lax.complex(qka * jnp.cos(qkp), qka * jnp.sin(qkp)), s=(P, P))
        out1 = _layernorm(_unpatch(out1), ln1_w, ln1_b)
        out2 = _layernorm(_unpatch(out2), ln2_w, ln2_b)
        out3 = _layernorm(_unpatch(out3), ln3_w, ln3_b)
        cat = jnp.concatenate([v_value * out1, v_value * out2, v_value * out3], axis=1)
        return jnp.einsum('bchw,oc->bohw', cat, w_proj)

    def _gn(v, G=32, eps=1e-5):
        B_, C_, H_, W_ = v.shape
        g = v.reshape(B_, G, C_ // G, H_, W_)
        m = jnp.mean(g, axis=(2, 3, 4), keepdims=True)
        s = jnp.var(g, axis=(2, 3, 4), keepdims=True)
        return ((g - m) / jnp.sqrt(s + eps)).reshape(v.shape)

    def _ln_c(v, eps=1e-6):
        m = jnp.mean(v, axis=1, keepdims=True)
        s = jnp.var(v, axis=1, keepdims=True)
        return (v - m) / jnp.sqrt(s + eps)

    def _ln_t(v, eps=1e-5):
        m = jnp.mean(v, axis=-1, keepdims=True)
        s = jnp.var(v, axis=-1, keepdims=True)
        return (v - m) / jnp.sqrt(s + eps)

    def _to_tokens(v):
        B_, C_, H_, W_ = v.shape
        return v.reshape(B_, C_, H_ * W_).transpose(0, 2, 1)
    def _from_tokens(t, like):
        B_, C_, H_, W_ = like.shape
        return t.transpose(0, 2, 1).reshape(B_, C_, H_, W_)

    x = x + _L0_conv_ref(_gn(x), L0_conv_conv1_w, L0_conv_conv1_b, L0_conv_dw1_w, L0_conv_dw1_b, L0_conv_dw2_w, L0_conv_dw2_b, L0_conv_dw3_w, L0_conv_dw3_b, L0_conv_pw_w, L0_conv_pw_b, L0_conv_ca_w1, L0_conv_ca_w2, L0_conv_sa_w, L0_conv_sa_b, L0_conv_gn_g, L0_conv_gn_b)
    x = x + _L1_conv_ref(_gn(x), L1_conv_w_hidden, L1_conv_w_dw, L1_conv_w_proj, L1_conv_fft_param, L1_conv_ln1_w, L1_conv_ln1_b, L1_conv_ln2_w, L1_conv_ln2_b, L1_conv_ln3_w, L1_conv_ln3_b)
    return x


_drawn_inputs = setup_inputs


def setup_inputs(seed=0):
    import zlib

    import numpy as np

    out = dict(_drawn_inputs(seed))
    spreads = {'L0_conv_conv1_b': (0.0, 0.8),
     'L0_conv_dw1_b': (0.0, 0.34),
     'L0_conv_dw2_b': (0.0, 0.311),
     'L0_conv_dw3_b': (0.0, 0.303),
     'L0_conv_pw_b': (0.0, 0.394),
     'L0_conv_gn_g': (1.0, 0.2),
     'L0_conv_gn_b': (0.0, 0.1),
     'L1_conv_fft_param': (1.0, 0.6),
     'L1_conv_ln1_w': (1.0, 0.6),
     'L1_conv_ln1_b': (0.0, 0.8),
     'L1_conv_ln2_w': (1.0, 0.6),
     'L1_conv_ln2_b': (0.0, 0.8),
     'L1_conv_ln3_w': (1.0, 0.6),
     'L1_conv_ln3_b': (0.0, 0.8)}
    factors = {'L0_conv_dw1_w': 4.031}
    for name, (base, spread) in spreads.items():
        noise = np.random.default_rng([zlib.crc32(name.encode()), seed]).standard_normal(out[name].shape)
        drawn = base * np.exp(spread * noise) if base else spread * noise
        out[name] = jnp.asarray(drawn.astype(out[name].dtype))
    for name, factor in factors.items():
        out[name] = (out[name] * factor).astype(out[name].dtype)
    return out
```

```python
import concourse.bass as bass
from concourse import mybir
from concourse.alu_op_type import AluOpType as ALU
from contextlib import ExitStack

F32 = mybir.dt.float32
ACT = mybir.ActivationFunctionType
AX = mybir.AxisListType

C, H, W = 64, 256, 256
RP = H // 2
UNITS = RP // 2
BODY = 4
HR = 8
E = 76
E4 = 4 * E
P = 8
NF = P * (P // 2 + 1)
NF2 = 2 * NF
BLK = 4
SBN = BLK * E
NSB = (H // P) * (W // (16 * BLK))
PROWS = H // P
SBROW = NSB // PROWS
LBODY = 8
THR = 1e-10
BIG = -3.0e38
BAND_LO, BAND_N = 96, 192
K0 = 131
GN_EPS = 1e-5


def build(nc, B, io, out):
    ctx = ExitStack()
    with ctx:
        def sb(name, shape):
            return ctx.enter_context(nc.sbuf_tensor(name, shape, F32))

        def sem(name):
            return ctx.enter_context(nc.semaphore(name))

        x_in = io["x"]
        band7d = nc.dram_tensor("band7_scratch", (128, 14 * BAND_N), F32).ap()
        x1d = nc.dram_tensor("x1_scratch", (B, C, H + 2, W), F32).ap()

        WORK = 5300
        AREA = 45600
        arena = sb("arena", [128, AREA])
        img = arena[:, 0:RP * W].rearrange("p (r w) -> p r w", w=W)
        work = arena[:, RP * W:RP * W + WORK]
        K5 = sb("K5", [128, 3, 5, 128])
        consts = sb("consts", [128, 130 + 4 * 128])
        diag130 = consts[:, 0:130]
        ident = consts[:, 0:128]
        avg2, avg8, avgq, swapq = (consts[:, 130 + 128 * k:258 + 128 * k] for k in range(4))
        ones_row = sb("ones_row", [1, 128])
        W1 = sb("W1", [128, 128])
        cols = sb("cols", [128, 64])
        b1 = cols[:, 0:1]
        cbias = cols[:, 1:2]
        gn_g, gn_b = cols[:, 2:3], cols[:, 3:4]
        sa_b = cols[:, 4:5]
        pwb = cols[:, 5:6]
        half_ln = cols[:, 6:7]
        caw1 = sb("caw1", [128, 8])
        caw2 = sb("caw2", [8, 128])
        saw = sb("saw", [128, 99])
        stats = sb("stats", [128, UNITS, 6])
        mxs = sb("mxs", [128, UNITS])
        sms = sb("sms", [128, UNITS])
        WA = sb("WA", [128, 3, E4])
        WB = sb("WB", [128, 2, E4])
        param = sb("param", [NF2, E])
        WP = sb("WP", [128, 3, C])
        FR = sb("FR", [128, NF2])
        FI = sb("FI", [128, NF2])
        GR = sb("GR", [NF2, 128])
        GI = sb("GI", [NF2, 128])

        hring = work[:, 0:HR * 260].rearrange("p (r w) -> p r w", w=260)
        yring = work[:, 2080:2080 + 4 * 512].rearrange("p (k n) -> p k n", k=4)
        zring = work[:, 4128:4128 + 2 * 512].rearrange("p (k n) -> p k n", k=2)
        cring = work[:, 0:2 * 512].rearrange("p (k n) -> p k n", k=2)
        saring = work[:, 2600:2600 + 2 * 512].rearrange("p (k h r c) -> p k h r c", k=2, h=2, r=4)
        band7 = work[:, 2600:2600 + 14 * BAND_N].rearrange("p (n u) -> p n u", n=14)
        maps = work[:, 1040:1040 + 4 * (H + 6)].rearrange("p (a h r) -> p a h r", a=2, h=2)
        sa = work[:, 2088:2088 + 2 * H].rearrange("p (h r) -> p h r", h=2)
        xring = work[:, 0:2 * 2048].rearrange("p (k n) -> p k n", k=2)
        gring = work[:, 4096:4096 + 2 * 512].rearrange("p (k n) -> p k n", k=2)
        padrow = sb("padrow", [64, W])

        used = [0]

        def carve(parts, n):
            a = arena[0:parts, used[0]:used[0] + n]
            used[0] += n
            return a

        xraw = carve(128, 2 * P * W).rearrange("p (a r w) -> p a r w", a=2, w=W)
        ynorm = carve(128, 2 * 2 * (W + 2) * P).rearrange("p (k a w r) -> p k a w r", k=2, a=2, r=P)
        stage = carve(128, P * W).rearrange("p (r w) -> p r w", w=W)
        ostage = (stage[0:64], stage[64:128])
        hdw = carve(128, 4 * BLK * E4).rearrange("p (k b n) -> p k b n", k=4, b=BLK)
        spec = carve(NF2, 2 * 8 * SBN).rearrange("p (k a n) -> p k a n", k=2, a=8)
        mask = carve(NF2, 8 * SBN).rearrange("p (a n) -> p a n", a=8)
        gspec = carve(NF2, 8 * SBN).rearrange("p (a n) -> p a n", a=8)
        prod = carve(NF2, 4 * SBN).rearrange("p (a n) -> p a n", a=4)
        pprod = carve(NF2, 4 * SBN).rearrange("p (a n) -> p a n", a=4)
        cross = carve(NF2, 2 * SBN).rearrange("p (a n) -> p a n", a=2)
        n2 = carve(NF2, 4 * SBN).rearrange("p (a n) -> p a n", a=4)
        lnn = carve(NF2, 4 * SBN).rearrange("p (a n) -> p a n", a=4)
        r0 = carve(NF2, 4 * SBN).rearrange("p (a n) -> p a n", a=4)
        pmag = carve(NF2, 6 * SBN).rearrange("p (a n) -> p a n", a=6)
        outs = carve(NF2, 6 * SBN).rearrange("p (a n) -> p a n", a=6)
        dev = carve(128, 3 * SBN).rearrange("p (j b e) -> p j b e", j=3, e=E)
        devsq = carve(128, 3 * SBN).rearrange("p (j b e) -> p j b e", j=3, e=E)
        cat = carve(128, 2 * BLK * E4).rearrange("p (k b n) -> p k b n", k=2, b=BLK)
        catT = carve(128, 3 * 512).rearrange("p (a n) -> p a n", a=3)
        lnst = carve(128, 8 * 12).rearrange("p (k n) -> p k n", k=8)
        assert used[0] <= AREA and RP * W + WORK <= AREA, used[0]
        used[0] = 0
        band7_new = carve(128, 14 * BAND_N).rearrange("p (n u) -> p n u", n=14)
        dense5 = carve(128, 25 * C).rearrange("p (t n) -> p t n", n=C)
        pwT = carve(128, 3 * C).rearrange("p (j n) -> p j n", j=3)
        dwc = carve(128, 35)
        dbc = carve(128, 3)
        bands = carve(128, 198)
        sarow = carve(1, 99)
        wdrow = carve(1, 9 * E4)
        wdb = carve(128, 9 * E4).rearrange("p (t n) -> p t n", t=9)
        whT = carve(128, E4)
        wp4 = carve(E, 4 * C).rearrange("p (j n) -> p j n", j=4)
        wpr = carve(E, 3 * C).rearrange("p (j n) -> p j n", j=3)
        lnw = carve(E, 3)
        lnb = carve(E, 3)

        psum = ctx.enter_context(nc.psum_tensor("psum", [128, 8, 512], F32))

        def bank(k):
            return psum[:, k, :]

        loaded = sem("setup_loaded")
        memset_done = sem("memset_done")
        v_setup = sem("v_setup")
        p_setup = sem("p_setup")
        wp4_done = sem("wp4_done")
        setup_done = sem("setup_done")
        band_stored = sem("band_stored")
        band_loaded = sem("band_loaded")
        packed = sem("packed")
        image_done = sem("image_done")
        x_in_sems = [sem(f"x_loaded{k}") for k in range(4)]
        stat_done = sem("x_stats")
        gn = sem("gn_small")
        gmm = sem("gn_matmul")
        gact = sem("gn_act")
        y_done = sem("y_done")
        c1_done = sem("conv1_done")
        h_done = sem("h_done")
        c5_done = sem("conv5_done")
        z_done = sem("z_done")
        zs_done = sem("z_plus_y")
        img_done = sem("h_image")
        red_done = sem("h_reduced")
        cp_done = sem("scaled_copy")
        tr_done = sem("transposed")
        map_done = sem("maps_done")
        sac_done = sem("sa_conv")
        sa_done = sem("sa_done")
        sar_done = sem("sa_rows")
        sab_done = sem("sa_broadcast")
        out2_done = sem("sa_ca_h")
        st2_done = sem("out_stats")
        xr_sems = [sem(f"x_again{k}") for k in range(2)]
        gs_done = sem("gn_silu")
        x1_done = sem("x1_done")
        st3_done = sem("x1_stats")
        x1_stored = [sem(f"x1_stored{k}") for k in range(2)]
        pad_done = sem("pad_row")
        pad_stored = sem("pad_stored")
        ln_ready = sem("layer1_ready")
        xp_done = sem("patch_rows_loaded")
        yp_done = sem("patch_rows_normalised")
        conv_done = sem("conv_done")
        hdw_done = sem("hdw_evacuated")
        dft_done = sem("dft_done")
        ft_done = sem("dft_evacuated")
        vpar_done = sem("v_times_param")
        qkp_done = sem("qk_products")
        qk_done = sem("qk_done")
        abs_done = sem("abs_all")
        mask_done = sem("guard_mask")
        guard_done = sem("guarded")
        sprod_done = sem("cross_products")
        cross_done = sem("cross_done")
        sq_done = sem("squares_done")
        n2_done = sem("norms2_done")
        rs_act = sem("rsqrt_act")
        rs_dve = sem("rsqrt_newton")
        mag_done = sem("magnitudes")
        amp_done = sem("amplitudes")
        outs_done = sem("outs_done")
        idft_done = sem("idft_done")
        sum_done = sem("ln_sum")
        dev_done = sem("ln_dev")
        dsq_done = sem("ln_devsq")
        var_done = sem("ln_var")
        vv_done = sem("ln_dev_vv")
        lr_act = sem("ln_rstd_act")
        lr_dve = sem("ln_rstd_newton")
        vcp_done = sem("vv_in_cat")
        cat_done = sem("cat_done")
        proj_done = sem("proj_done")
        os_sems = [sem(f"residual_loaded{k}") for k in range(2)]
        res_done = sem("residual_added")
        st_sems = [sem(f"out_stored{k}") for k in range(2)]

        block = ctx.enter_context(nc.Block())

        def unit(t):
            return img[:, bass.ds(2 * t, 2), :]

        def pairs(a):
            return a.rearrange("p (r w) -> p r w", w=W)

        def bc(a, n):
            return a.unsqueeze(len(a.shape)).to_broadcast(list(a.shape) + [n])

        def bodies(eng, step, n_steps, lag, size):
            for m in range(PEEL):
                step(m, m, m // size)
            with eng.Fori(PEEL // size, n_steps // size) as i:
                for u in range(size):
                    step(i * size + u, PEEL + u, i)
            for m in range(n_steps, n_steps + lag):
                step(m, m, m // size)

        PEEL = 8
        N0 = UNITS
        N_CHUNKS = RP // 8
        USES = 9 * NSB
        G_V, G_A, G_M = 26, 5, 10
        rows3 = (128, 128, E4 - 256)

        def use(n, t, k):
            return 6 * n + k if t < 3 else 9 * n - 9 + k

        def tuse(m, s, k):
            return 9 * m - 3 + k if s < NSB else 9 * NSB - 9 + 3 * (m - NSB) + k

        loads = [
            (consts[:, :], io["consts"]), (bands, io["bands"]),
            (FR[:, :], io["FR"]), (FI[:, :], io["FI"]), (GR[:, :], io["GR"]), (GI[:, :], io["GI"]),
            (b1[0:64], io["conv1_b"]), (b1[64:128], io["conv1_b"]),
            (gn_g[0:64], io["gn_g"]), (gn_g[64:128], io["gn_g"]),
            (gn_b[0:64], io["gn_b"]), (gn_b[64:128], io["gn_b"]),
            (pwb[0:64], io["pw_b"]), (pwb[64:128], io["pw_b"]),
            (pwT[0:64], io["pwT"]), (pwT[64:128], io["pwT"]),
            (dwc[0:64], io["dwc"]), (dwc[64:128], io["dwc"]),
            (dbc[0:64], io["dbc"]),
            (caw1[0:64, :], io["caw1T"]), (caw2[:, 0:64], io["caw2T"]), (caw2[:, 64:128], io["caw2T"]),
            (sarow, io["sarow"]), (wdrow, io["wdrow"]),
            (whT[0:64], io["whT"]), (whT[64:128], io["whT"]),
            (param[0:NF, :], io["param"]), (param[NF:NF2, :], io["param"]),
            (wpr, io["wpT"]), (lnw, io["lnw"]), (lnb, io["lnb"]),
            (W1[0:64, 0:64], io["w1T"]), (W1[64:128, 64:128], io["w1T"]),
        ]
        packs = []
        for a_ in range(4):
            done_ = 0
            while done_ < E:
                row_ = a_ * E + done_
                n_ = min(E - done_, 128 - row_ % 128)
                packs.append((WP[row_ % 128:row_ % 128 + n_, row_ // 128, :], wp4[done_:done_ + n_, a_, :]))
                done_ += n_

        @block.sync
        def _(sp):
            sp.wait_ge(memset_done, 1)
            for dst, src in loads:
                sp.dma_start(dst, src).then_inc(loaded, 16)
            sp.wait_ge(wp4_done, 1)
            for dst, src in packs:
                sp.dma_start(dst, src).then_inc(packed, 16)
            sp.wait_ge(setup_done, 1)
            sp.dma_start(band7d, band7_new.rearrange("p n u -> p (n u)")).then_inc(band_stored, 16)
            sp.wait_ge(band_stored, 16)
            sp.wait_ge(packed, 16 * len(packs))
            sp.sem_inc(image_done, 1)
            with sp.Fori(0, B) as b:
                sp.wait_ge(image_done, b + 1)
                xv = x_in[bass.ds(b, 1)].rearrange("o c (i q) w -> (o q) c i w", q=2)

                def load_x(i):
                    for k in range(4):
                        for q in range(2):
                            sp.dma_start(img[64 * q:64 * q + 64, bass.ds(i * 32 + 8 * k, 8), :],
                                         xv[q, :, bass.ds(i * 32 + 8 * k, 8), :]).then_inc(x_in_sems[k], 16)

                load_x(0)
                with sp.Fori(1, N_CHUNKS // 4) as i:
                    sp.wait_ge(stat_done, b * UNITS + i * 16)
                    load_x(i)

                sp.wait_ge(red_done, b * UNITS + UNITS)
                sp.dma_start(band7.rearrange("p n u -> p (n u)"), band7d).then_inc(band_loaded, 16)

                x1v = x1d[bass.ds(b, 1), :, 1:H + 1, :].rearrange("o c (i q) w -> (o q) c i w", q=2)

                def load_again(j, k):
                    for q in range(2):
                        sp.dma_start(pairs(xring[64 * q:64 * q + 64, k, :]),
                                     xv[q, :, bass.ds(j * 8, 8), :]).then_inc(xr_sems[k], 16)

                def store_x1(j, k):
                    sp.wait_ge(x1_done, b * UNITS + j * 4 + 4)
                    for q in range(2):
                        sp.dma_start(x1v[q, :, bass.ds(j * 8, 8), :],
                                     pairs(xring[64 * q:64 * q + 64, k, :])).then_inc(x1_stored[k], 16)

                sp.wait_ge(out2_done, b * UNITS + UNITS)
                load_again(0, 0)
                load_again(1, 1)
                with sp.Fori(0, N_CHUNKS // 2 - 1) as i:
                    for k in range(2):
                        store_x1(i * 2 + k, k)
                        sp.wait_ge(st3_done, b * UNITS + i * 8 + (4 * k + 4))
                        sp.wait_ge(x1_stored[k], b * 256 + i * 32 + 32)
                        load_again(i * 2 + (k + 2), k)
                for k in range(2):
                    store_x1(N_CHUNKS - 2 + k, k)
                sp.wait_ge(pad_done, b + 1)
                for k in range(2):
                    sp.wait_ge(x1_stored[k], b * 256 + 256)
                for r in (H + 1, 0):
                    sp.dma_start(x1d[bass.ds(b, 1), :, r:r + 1, :].rearrange("o c r w -> (o c) (r w)"),
                                 padrow[:, :]).then_inc(pad_stored, 16)
                sp.wait_ge(pad_stored, b * 32 + 32)
                sp.wait_ge(ln_ready, b + 1)
                sv = x1d[bass.ds(b, 1)].rearrange("o c r w -> (o c) r w")
                ov = out[bass.ds(b, 1)].rearrange("o c r w -> (o c) r w")

                def load_rows(j):
                    for half, a, dy in ((0, 0, 0), (1, 0, 1), (0, 1, 2), (1, 1, 2)):
                        sp.dma_start(xraw[64 * half:64 * half + 64, a],
                                     sv[:, bass.ds(j * 8 + dy, 8), :]).then_inc(xp_done, 16)

                def store_rows(j, k):
                    sp.wait_ge(res_done, b * NSB + j * SBROW + SBROW)
                    sp.dma_start(ov[:, bass.ds(j * 8, 8), :], ostage[k]).then_inc(st_sems[k], 16)

                def load_residual(j, k):
                    sp.dma_start(ostage[k], sv[:, bass.ds(j * 8 + 1, 8), :]).then_inc(os_sems[k], 16)

                load_rows(0)
                for k in range(2):
                    load_residual(k, k)
                sp.wait_ge(yp_done, b * PROWS + 1)
                load_rows(1)
                with sp.Fori(1, PROWS // 2) as i:
                    for k in range(2):
                        sp.wait_ge(yp_done, b * PROWS + i * 2 + k)
                        load_rows(i * 2 + k)
                        store_rows(i * 2 + (k - 2), k)
                        sp.wait_ge(st_sems[k], b * 256 + i * 16)
                        load_residual(i * 2 + k, k)
                for k in range(2):
                    store_rows(PROWS - 2 + k, k)
                for k in range(2):
                    sp.wait_ge(st_sems[k], b * 256 + 256)
                sp.sem_inc(image_done, 1)

        @block.tensor
        def _(pe):
            mm = nc.tensor.matmul
            pe.wait_ge(loaded, 16 * len(loads))
            pe.wait_ge(memset_done, 2)
            for q in range(2):
                for j in range(3):
                    last = mm(psum[64 * q:64 * q + 64, 0, 0:1], pwT[0:64, j, :], dbc[0:64, j:j + 1],
                              start=(j == 0), stop=(j == 2))
            last.then_inc(p_setup, 1)
            mm(psum[:, 1, 0:99], ones_row[:, :], sarow, start=True, stop=True).then_inc(p_setup, 1)
            for k in range(6):
                mm(psum[:, 2 + k, 0:456], ones_row[:, :], wdrow[:, 456 * k:456 * k + 456],
                   start=True, stop=True).then_inc(p_setup, 1)
            pe.wait_ge(setup_done, 1)
            pe.wait_ge(packed, 16 * len(packs))

            with pe.Fori(0, B) as b:
                pe.wait_ge(image_done, b + 1)

                def stat(matrix, rhs, need):
                    pe.wait_ge(gn, b * G_V + need)
                    mm(psum[:, 7, 0:1], matrix, rhs, start=True, stop=True).then_inc(gmm, 1)

                mean_col, var_col = cols[:, 16:17], cols[:, 20:21]
                stat(avg2, mean_col, 1)
                stat(avg2, var_col, 4)

                def convs(m, s, g):
                    if s < N0:
                        pe.wait_ge(y_done, b * UNITS + m + 1)
                        if s >= 2:
                            pe.wait_ge(h_done, b * UNITS + m - 1)
                        mm(bank(s % 2), W1[:, :], yring[:, s % 4, :], start=True, stop=True).then_inc(c1_done, 1)
                    t = s - 2
                    if t < 0:
                        return
                    pe.wait_ge(h_done, b * UNITS + (m if t < N0 - 1 else m - 1))
                    if t >= 2:
                        pe.wait_ge(z_done, b * UNITS + m - 3)
                    o = 2 + t % 2
                    terms = []
                    for e, taps in ((0, range(4)), (-1, range(5)), (1, range(5)), (0, (4,))):
                        rows = [2 * t + r + e for r in range(2)]
                        inside = [0 <= r < RP for r in rows]
                        at = [r % HR for r in rows]
                        for dx in taps:
                            if all(inside) and at[1] == at[0] + 1:
                                terms.append((e, dx, 0, 2, at[0]))
                            else:
                                terms += [(e, dx, r, 1, at[r]) for r in range(2) if inside[r]]
                    for n, (e, dx, r, k, at) in enumerate(terms):
                        last = mm(psum[:, o, 256 * r:256 * (r + k)], K5[:, e + 1, dx, :],
                                  hring[:, at:at + k, dx:dx + W], start=(n == 0),
                                  stop=(n == len(terms) - 1), skip_group_check=(k == 1))
                    last.then_inc(c5_done, 1)

                bodies(pe, convs, N0, 2, BODY)

                stat(avgq, cols[:, 24:25], 8)
                stat(swapq, cols[:, 25:26], 9)
                pe.wait_ge(gn, b * G_V + 10)
                mm(psum[0:8, 7, 0:2], caw1[:, :], cols[:, 26:28], start=True, stop=True).then_inc(gmm, 1)
                pe.wait_ge(gact, b * G_A + 2)
                mm(psum[:, 7, 0:2], caw2[:, :], cols[0:8, 28:30], start=True, stop=True).then_inc(gmm, 1)

                def transposes(m, s, g):
                    pe.wait_ge(cp_done, b * UNITS + m + 1)
                    if s >= 2:
                        pe.wait_ge(map_done, b * UNITS + m - 1)
                    for r in range(2):
                        for hf in range(2):
                            last = mm(psum[:, 2 * (s % 2) + r, 130 * hf:130 * hf + 130],
                                      cring[:, s % 2, 256 * r + 128 * hf:256 * r + 128 * hf + 128],
                                      diag130, start=True, stop=True)
                    last.then_inc(tr_done, 1)

                bodies(pe, transposes, N0, 0, BODY)

                pe.wait_ge(map_done, b * UNITS + UNITS)
                pe.wait_ge(band_loaded, b * 16 + 16)
                for ho in range(2):
                    hi = 1 - ho
                    p0, u0 = (96, 96) if hi == 1 else (0, 256)
                    for n in range(14):
                        a, dy = n // 7, n % 7
                        mm(psum[:, 4, 256 * ho:256 * ho + 256], band7[:, n, 128 - BAND_LO:256 - BAND_LO],
                           maps[:, a, ho, dy:dy + H], start=(n == 0), stop=(n == 13))
                    for n in range(14):
                        a, dy = n // 7, n % 7
                        last = mm(psum[p0:p0 + 32, 4, 256 * ho:256 * ho + 256],
                                  band7[:, n, u0 - BAND_LO:u0 + 32 - BAND_LO],
                                  maps[:, a, hi, dy:dy + H], start=False, stop=(n == 13), skip_group_check=True)
                last.then_inc(sac_done, 1)

                def spread(m, s, g):
                    pe.wait_ge(sar_done, b * UNITS + m + 1)
                    if s >= 2:
                        pe.wait_ge(out2_done, b * UNITS + m - 1)
                    for r in range(2):
                        for hf in range(2):
                            last = mm(psum[:, 5 + s % 2, 256 * r + 128 * hf:256 * r + 128 * hf + 128],
                                      saring[:, s % 2, hf, 2 * r:2 * r + 2, :].rearrange("p q c -> p (q c)"), ident,
                                      start=True, stop=True)
                    last.then_inc(sab_done, 1)

                bodies(pe, spread, N0, 0, BODY)
                stat(avg8, mean_col, 12)
                stat(avg8, var_col, 15)
                stat(avg2, mean_col, 21)
                stat(avg2, var_col, 24)

                pe.wait_ge(ln_ready, b + 1)

                def idft(n, t):
                    pe.wait_ge(outs_done, b * NSB + n + 1)
                    for j in range(3):
                        if 3 * t + j >= 2:
                            pe.wait_ge(dev_done, b * 3 * NSB + 3 * n + (j - 1))
                        o = psum[:, 5 + (3 * t + j) % 2, 0:SBN]
                        mm(o, GR[:, :], outs[:, 2 * j, :], start=True, stop=False)
                        mm(o, GI[:, :], outs[:, 2 * j + 1, :], start=False, stop=True).then_inc(idft_done, 1)

                def conv(n, t, row):
                    k = (t // SBROW) % 2
                    if t % SBROW == 0:
                        pe.wait_ge(yp_done, b * PROWS + row + 1)
                    for q in range(BLK):
                        if 4 * t + q >= 2:
                            pe.wait_ge(hdw_done, b * 4 * NSB + 4 * n + (q - 1))
                        c0 = 64 * (t % SBROW) + 16 * q
                        o = psum[:, q % 2, 0:E4]

                        def pixels(half, a, dx):
                            return ynorm[0:64 * half, k, a, c0 + dx:c0 + dx + 16, :].rearrange("p w r -> p (w r)")

                        for dx in range(3):
                            mm(o, pixels(2, 0, dx), WA[:, dx, :], start=(dx == 0), stop=False)
                        mm(o, pixels(2, 1, 0), WB[:, 0, :], start=False, stop=False)
                        mm(o, pixels(1, 1, 2), WB[0:64, 1, :], start=False, stop=True).then_inc(conv_done, 1)

                def dft(n, t):
                    pe.wait_ge(hdw_done, b * 4 * NSB + 4 * n + 4)
                    for k in range(6):
                        if 6 * t + k >= 3:
                            pe.wait_ge(ft_done, b * USES + use(n, t, k) - 2)
                        mm(psum[0:NF2, 2 + k % 3, 0:SBN], (FR, FI)[k % 2][:, :],
                           hdw[:, t % 4, :, (k // 2) * E:(k // 2) * E + E],
                           start=True, stop=True).then_inc(dft_done, 1)

                def project(n, t, m, s):
                    pe.wait_ge(cat_done, b * NSB + n + 1)
                    pe.wait_ge(vcp_done, b * NSB + n + 1)
                    for k, rows in enumerate(rows3):
                        pe.wait_ge(ft_done, b * USES + tuse(m, s, k) - 2)
                        for q in range(BLK):
                            last = mm(psum[0:rows, 2 + k, 128 * q:128 * q + 128],
                                      cat[:, t % 2, q, 128 * k:128 * k + rows], ident, start=True, stop=True)
                        last.then_inc(dft_done, 1)
                    if t >= 1:
                        pe.wait_ge(res_done, b * NSB + n)
                    pe.wait_ge(ft_done, b * USES + tuse(m, s, 2) + 1)
                    for k, rows in enumerate(rows3):
                        last = mm(psum[0:64, 7, :], WP[0:rows, k, :], catT[0:rows, k, :],
                                  start=(k == 0), stop=(k == 2))
                    last.then_inc(proj_done, 1)

                def layer1(m, s, g):
                    if 2 <= s < NSB + 2:
                        idft(m - 2, s - 2)
                    if s < NSB:
                        conv(m, s, m // SBROW if isinstance(m, int) else g * 2 + (s % LBODY) // SBROW)
                        dft(m, s)
                    if s >= 3:
                        project(m - 3, s - 3, m, s)

                bodies(pe, layer1, NSB, 3, LBODY)

        @block.scalar
        def _(act):
            fn = nc.scalar.activation
            with act.Fori(0, B) as b:
                act.wait_ge(image_done, b + 1)

                def root(k, need):
                    act.wait_ge(gn, b * G_V + need)
                    fn(cols[:, 22:23], cols[:, 21:22], ACT.Sqrt).then_inc(gact, 1)

                root(1, 5)

                def silus(m, s, g):
                    if s < N0:
                        act.wait_ge(c1_done, b * UNITS + m + 1)
                        if s >= 4:
                            act.wait_ge(c5_done, b * UNITS + m - 2)
                        r = (2 * s) % HR
                        fn(hring[:, r:r + 2, 2:2 + W], pairs(bank(s % 2)), ACT.Silu,
                           bias=b1).then_inc(h_done, 1)
                    if 3 <= s < N0 + 3:
                        t = s - 3
                        act.wait_ge(c5_done, b * UNITS + m - 2)
                        if t >= 2:
                            act.wait_ge(img_done, b * UNITS + m - 4)
                        fn(zring[:, t % 2, :], bank(2 + t % 2), ACT.Silu, bias=cbias).then_inc(z_done, 1)
                    if s >= 4:
                        act.wait_ge(zs_done, b * UNITS + m - 3)
                        fn(unit(m - 4), pairs(zring[:, (s - 4) % 2, :]), ACT.Silu).then_inc(img_done, 1)

                bodies(act, silus, N0, 4, BODY)

                act.wait_ge(gmm, b * G_M + 5)
                fn(cols[0:8, 28:30], psum[0:8, 7, 0:2], ACT.Relu).then_inc(gact, 1)
                act.wait_ge(gn, b * G_V + 11)
                ca = cols[:, 31:32]
                fn(ca, cols[:, 30:31], ACT.Silu).then_inc(gact, 1)
                act.wait_ge(gact, b * G_A + 3)

                def scaled(m, s, g):
                    if s >= 2:
                        act.wait_ge(tr_done, b * UNITS + m - 1)
                    fn(pairs(cring[:, s % 2, :]), unit(m), ACT.Copy, scale=ca).then_inc(cp_done, 1)

                bodies(act, scaled, N0, 0, BODY)

                act.wait_ge(sac_done, b + 1)
                fn(sa[:, :, :], psum[:, 4, :].rearrange("p (h n) -> p h n", h=2), ACT.Silu,
                   bias=sa_b).then_inc(sa_done, 1)

                act.wait_ge(sa_done, b + 1)

                def sa_rows(m, s, g):
                    if s >= 2:
                        act.wait_ge(sab_done, b * UNITS + m - 1)
                    fn(saring[:, s % 2],
                       bc(sa[:, :, bass.ds(m * 4, 4)], 64), ACT.Copy).then_inc(sar_done, 1)

                bodies(act, sa_rows, N0, 0, BODY)

                root(4, 16)
                act.wait_ge(gn, b * G_V + 20)

                def gn_silu(m, s, g):
                    if s >= 2:
                        act.wait_ge(x1_done, b * UNITS + m - 1)
                    fn(pairs(gring[:, s % 2, :]), unit(m), ACT.Silu, bias=cols[:, 34:35],
                       scale=cols[:, 32:33]).then_inc(gs_done, 1)

                bodies(act, gn_silu, N0, 0, BODY)
                root(5, 25)

                act.wait_ge(ln_ready, b + 1)

                def evacuate(n, t, q):
                    act.wait_ge(conv_done, b * 4 * NSB + 4 * n + (q + 1))
                    if t >= 4 and q == 0:
                        act.wait_ge(vv_done, b * NSB + n - 3)
                        act.wait_ge(vcp_done, b * NSB + n - 3)
                    fn(hdw[:, t % 4, q, :], psum[:, q % 2, 0:E4], ACT.Copy).then_inc(hdw_done, 1)

                def layer1(m, s, g):
                    n, t, k = m - 1, s - 1, (s - 1) % 2
                    if 0 <= t < NSB:
                        act.wait_ge(vpar_done, b * NSB + n + 1)
                        act.wait_ge(qk_done, b * NSB + n + 1)
                        if t >= 1:
                            act.wait_ge(n2_done, b * NSB + n)
                        fn(mask, spec[:, k], ACT.Abs).then_inc(abs_done, 1)
                    if s < NSB:
                        evacuate(m, s, 0)
                        evacuate(m, s, 1)
                    if 0 <= t < NSB:
                        act.wait_ge(guard_done, b * NSB + n + 1)
                        fn(mask, gspec, ACT.Square).then_inc(sq_done, 1)
                    if 2 <= s < NSB + 2:
                        if s >= 4:
                            act.wait_ge(proj_done, b * NSB + m - 3)
                        fn(cat[:, s % 2, :, 3 * E:E4], hdw[:, (s - 2) % 4, :, 3 * E:E4],
                           ACT.Copy).then_inc(vcp_done, 1)
                    if s < NSB:
                        evacuate(m, s, 2)
                        evacuate(m, s, 3)
                    if 0 <= t < NSB:
                        act.wait_ge(n2_done, b * NSB + n + 1)
                        if t >= 1:
                            act.wait_ge(rs_dve, b * 2 * NSB + 2 * n)
                        base = b * 3 * NSB + 3 * n
                        fn(lnn[:, :, :], n2[:, :, :], ACT.Ln, scale=65536.0).then_inc(rs_act, 1)
                        act.wait_ge(rs_act, base + 1)
                        fn(r0[:, :, :], lnn[:, :, :], ACT.Exp, scale=-0.5, bias=half_ln[0:NF2]).then_inc(rs_act, 1)
                        act.wait_ge(rs_act, base + 2)
                        fn(lnn[:, :, :], r0[:, :, :], ACT.Square).then_inc(rs_act, 1)
                    if 2 <= s < NSB + 2:
                        base = b * 3 * NSB + 3 * m - 6
                        for j in range(3):
                            act.wait_ge(dev_done, base + (j + 1))
                            fn(devsq[:, j], dev[:, j], ACT.Square).then_inc(dsq_done, 1)
                        act.wait_ge(var_done, b * 2 * NSB + 2 * m - 2)
                        fn(lnst[:, 2, :], lnst[:, 1, :], ACT.Ln).then_inc(lr_act, 1)
                        act.wait_ge(lr_act, base + 1)
                        fn(lnst[:, 3, :], lnst[:, 2, :], ACT.Exp, scale=-0.5).then_inc(lr_act, 1)
                        act.wait_ge(lr_act, base + 2)
                        fn(lnst[:, 4, :], lnst[:, 3, :], ACT.Square).then_inc(lr_act, 1)
                    if s < NSB:
                        k = s % 2
                        if s >= 2:
                            act.wait_ge(guard_done, b * NSB + m - 1)
                        for c in range(6):
                            act.wait_ge(dft_done, b * USES + use(m, s, c) + 1)
                            fn(spec[:, k, c, :], psum[0:NF2, 2 + c % 3, 0:SBN], ACT.Copy).then_inc(ft_done, 1)
                    if s >= 3:
                        for c, rows in enumerate(rows3):
                            act.wait_ge(dft_done, b * USES + tuse(m, s, c) + 1)
                            if s >= 4 and c == 0:
                                act.wait_ge(proj_done, b * NSB + m - 3)
                            fn(catT[0:rows, c, :], psum[0:rows, 2 + c, :], ACT.Copy).then_inc(ft_done, 1)

                bodies(act, layer1, NSB, 3, LBODY)

        @block.gpsimd
        def _(pool):
            tt = nc.gpsimd.tensor_tensor
            with pool.Fori(0, B) as b:
                pool.wait_ge(ln_ready, b + 1)

                def layer1(m, s, g):
                    n, t = m - 1, s - 1
                    if 0 <= t < NSB:
                        pool.wait_ge(sq_done, b * NSB + n + 1)
                        if t >= 1:
                            pool.wait_ge(mag_done, b * NSB + n)
                        sv = mask.rearrange("p (a c) n -> p a c n", c=2)
                        tt(n2[:, :, :], sv[:, :, 0, :], sv[:, :, 1, :], ALU.add).then_inc(n2_done, 1)
                    if s < NSB:
                        k = s % 2
                        pool.wait_ge(ft_done, b * USES + use(m, s, 3) + 1)
                        tt(pprod[:, 0:2, :], spec[:, k, 0:2, :], spec[:, k, 2:4, :], ALU.mult)
                        tt(pprod[:, 2, :], spec[:, k, 0, :], spec[:, k, 3, :], ALU.mult)
                        tt(pprod[:, 3, :], spec[:, k, 1, :], spec[:, k, 2, :], ALU.mult).then_inc(qkp_done, 1)
                        pool.wait_ge(ft_done, b * USES + use(m, s, 5) + 1)
                        v = spec[:, k, 4:6, :].rearrange("p a (b e) -> p (a b) e", e=E)
                        tt(v, v, param[:, :].unsqueeze(1).to_broadcast([NF2, 2 * BLK, E]),
                           ALU.mult).then_inc(vpar_done, 1)
                        pool.wait_ge(qkp_done, b * NSB + m + 1)
                        tt(spec[:, k, 6, :], pprod[:, 0, :], pprod[:, 1, :], ALU.subtract)
                        tt(spec[:, k, 7, :], pprod[:, 2, :], pprod[:, 3, :], ALU.add).then_inc(qk_done, 1)

                bodies(pool, layer1, NSB, 1, LBODY)

        @block.vector
        def _(dve):
            v = nc.vector
            v.memset(caw1[:, :], 0.0)
            v.memset(W1[:, :], 0.0).then_inc(memset_done, 1)
            v.memset(half_ln, 5.545177444479562)
            v.memset(K5[:, :, :, :], 0.0)
            v.memset(band7_new, 0.0)
            v.memset(ones_row[:, :], 1.0).then_inc(memset_done, 1)
            dve.wait_ge(memset_done, 2)
            dve.wait_ge(loaded, 16 * len(loads))
            steps = [0]

            def link(ins):
                steps[0] += 1
                ins.then_inc(v_setup, 1)
                dve.wait_ge(v_setup, steps[0])

            dve.wait_ge(p_setup, 8)
            link(v.tensor_tensor(cbias, psum[:, 0, 0:1], pwb, ALU.add))
            link(v.tensor_copy(saw[:, :], psum[:, 1, 0:99]))
            link(v.tensor_copy(sa_b, saw[:, 98:99]))
            for k in range(6):
                v.tensor_copy(wdb.rearrange("p t n -> p (t n)")[:, 456 * k:456 * k + 456], psum[:, 2 + k, 0:456])
            for tap in range(25):
                v.tensor_scalar(dense5[:, tap, :], pwT[:, 2, :], dwc[:, 10 + tap:11 + tap], None, ALU.mult)
            link(v.memset(padrow[:, :], 0.0))
            for tap in range(9):
                at = (tap // 3 + 1) * 5 + tap % 3 + 1
                v.scalar_tensor_tensor(dense5[:, at, :], pwT[:, 1, :], dwc[:, 1 + tap:2 + tap],
                                       dense5[:, at, :], ALU.mult, ALU.add)
            link(v.memset(padrow[:, :], 0.0))
            link(v.scalar_tensor_tensor(dense5[:, 12, :], pwT[:, 0, :], dwc[:, 0:1],
                                        dense5[:, 12, :], ALU.mult, ALU.add))
            for e in (-1, 0, 1):
                for qi in range(2):
                    for qo in range(2):
                        dy = 2 * e + qi - qo
                        if -2 <= dy <= 2:
                            v.tensor_copy(K5[64 * qi:64 * qi + 64, e + 1, :, 64 * qo:64 * qo + 64],
                                          dense5[64 * qi:64 * qi + 64, 5 * (dy + 2):5 * (dy + 2) + 5, :])
            for dx in range(7):
                for n in range(14):
                    ins = v.scalar_tensor_tensor(band7_new[:, n, :], bands[:, dx:dx + BAND_N],
                                                 saw[:, 7 * n + dx:7 * n + dx + 1], band7_new[:, n, :],
                                                 ALU.mult, ALU.add)
                link(ins)
            for dx in range(3):
                for q in range(2):
                    v.tensor_tensor(WA[64 * q:64 * q + 64, dx, :], whT[64 * q:64 * q + 64],
                                    wdb[64 * q:64 * q + 64, 3 * q + dx, :], ALU.mult)
            for q in range(2):
                v.tensor_tensor(WB[64 * q:64 * q + 64, 0, :], whT[64 * q:64 * q + 64],
                                wdb[64 * q:64 * q + 64, 6 + q, :], ALU.mult)
            v.tensor_tensor(WB[0:64, 1, :], whT[0:64], wdb[0:64, 8, :], ALU.mult)
            for j in range(3):
                v.tensor_scalar(wp4[:, j, :], wpr[:, j, :], lnw[:, j:j + 1], None, ALU.mult)
            link(v.tensor_scalar(wp4[:, 3, :], wpr[:, 0, :], lnb[:, 0:1], None, ALU.mult))
            for j in (1, 2):
                link(v.scalar_tensor_tensor(wp4[:, 3, :], wpr[:, j, :], lnb[:, j:j + 1], wp4[:, 3, :],
                                            ALU.mult, ALU.add))
            v.memset(padrow[:, :], 0.0).then_inc(wp4_done, 1)
            dve.wait_ge(wp4_done, 1)
            v.memset(padrow[:, :], 0.0).then_inc(setup_done, 1)

            with dve.Fori(0, B) as b:
                dve.wait_ge(image_done, b + 1)
                at = [0]

                def small(ins):
                    at[0] += 1
                    ins.then_inc(gn, 1)
                    dve.wait_ge(gn, b * G_V + at[0])

                def group_norm(st, mm0, acts):
                    v.memset(cols[:, 45:46], 0.0)
                    small(v.bn_aggr(cols[:, 16:18], st))
                    dve.wait_ge(gmm, b * G_M + mm0 + 1)
                    small(v.tensor_copy(cols[:, 18:19], psum[:, 7, 0:1]))
                    small(v.tensor_tensor(cols[:, 19:20], cols[:, 16:17], cols[:, 18:19], ALU.subtract))
                    small(v.scalar_tensor_tensor(cols[:, 20:21], cols[:, 19:20], cols[:, 19:20],
                                                 cols[:, 17:18], ALU.mult, ALU.add))
                    dve.wait_ge(gmm, b * G_M + mm0 + 2)
                    small(v.tensor_scalar(cols[:, 21:22], psum[:, 7, 0:1], GN_EPS, None, ALU.add))
                    dve.wait_ge(gact, b * G_A + acts)
                    small(v.reciprocal(cols[:, 23:24], cols[:, 22:23]))

                v.memset(hring[:, :, 0:2], 0.0)
                v.memset(hring[:, :, 258:260], 0.0)
                with dve.Fori(0, N_CHUNKS // 4) as i:
                    for k in range(4):
                        dve.wait_ge(x_in_sems[k], b * 128 + i * 32 + 32)
                        for u in range(4):
                            t = i * 16 + (4 * k + u)
                            v.bn_stats(stats[:, bass.ds(t, 1), :],
                                       img[:, bass.ds(t * 2, 2), :]).then_inc(stat_done, 1)
                dve.wait_ge(stat_done, b * UNITS + UNITS)
                group_norm(stats[:, :, :], 0, 1)

                mean, rstd, ca = cols[:, 18:19], cols[:, 23:24], cols[:, 31:32]

                def mix(m, s, g):
                    if s < N0:
                        if s >= 4:
                            dve.wait_ge(c1_done, b * UNITS + m - 3)
                            dve.wait_ge(zs_done, b * UNITS + m - 3)
                        v.tensor_scalar(pairs(yring[:, s % 4, :]), unit(m), mean, rstd,
                                        ALU.subtract, ALU.mult).then_inc(y_done, 1)
                    if 3 <= s < N0 + 3:
                        t = s - 3
                        dve.wait_ge(z_done, b * UNITS + m - 2)
                        v.tensor_tensor(zring[:, t % 2, :], zring[:, t % 2, :], yring[:, t % 4, :],
                                        ALU.add).then_inc(zs_done, 1)
                    if s >= 5:
                        dve.wait_ge(img_done, b * UNITS + m - 4)
                        v.tensor_reduce(mxs[:, bass.ds(m - 5, 1)], unit(m - 5), AX.XY, ALU.max)
                        v.tensor_reduce(sms[:, bass.ds(m - 5, 1)], unit(m - 5), AX.XY,
                                        ALU.add).then_inc(red_done, 1)

                bodies(dve, mix, N0, 5, BODY)
                dve.wait_ge(red_done, b * UNITS + UNITS)
                small(v.tensor_reduce(cols[:, 24:25], sms[:, :], AX.X, ALU.add))
                small(v.tensor_reduce(cols[:, 25:26], mxs[:, :], AX.X, ALU.max))
                dve.wait_ge(gmm, b * G_M + 3)
                small(v.tensor_copy(cols[:, 26:27], psum[:, 7, 0:1]))
                dve.wait_ge(gmm, b * G_M + 4)
                small(v.tensor_tensor(cols[:, 27:28], psum[:, 7, 0:1], cols[:, 25:26], ALU.max))
                dve.wait_ge(gmm, b * G_M + 6)
                small(v.tensor_reduce(cols[:, 30:31], psum[:, 7, 0:2], AX.X, ALU.add))

                v.memset(maps[:, :, :, 0:3], 0.0)
                v.memset(maps[:, :, :, H + 3:H + 6], 0.0)

                def reduce_maps(m, s, g):
                    dve.wait_ge(tr_done, b * UNITS + m + 1)
                    for r in range(2):
                        o = psum[:, 2 * (s % 2) + r, 0:260].rearrange("p (h n) -> p h n", h=2)
                        rows = bass.ds(m * 4 + (2 * r + 3), 2)
                        v.tensor_reduce(maps[:, 1, :, rows], o[:, :, 0:128].rearrange("p h (q c) -> p h q c", q=2),
                                        AX.X, ALU.max)
                        last = v.tensor_copy(maps[:, 0, :, rows], o[:, :, 128:130])
                    last.then_inc(map_done, 1)

                bodies(dve, reduce_maps, N0, 0, BODY)

                dve.wait_ge(gact, b * G_A + 3)

                def apply(m, s, g):
                    dve.wait_ge(sab_done, b * UNITS + m + 1)
                    v.scalar_tensor_tensor(unit(m), unit(m), ca, pairs(psum[:, 5 + s % 2, :]),
                                           ALU.mult, ALU.mult).then_inc(out2_done, 1)
                    dve.wait_ge(out2_done, b * UNITS + m + 1)
                    v.bn_stats(stats[:, bass.ds(m, 1), :], unit(m)).then_inc(st2_done, 1)

                bodies(dve, apply, N0, 0, BODY)
                dve.wait_ge(st2_done, b * UNITS + UNITS)
                group_norm(stats[:, :, :], 6, 4)
                small(v.tensor_tensor(cols[:, 32:33], cols[:, 23:24], gn_g, ALU.mult))
                small(v.tensor_tensor(cols[:, 33:34], cols[:, 18:19], cols[:, 32:33], ALU.mult))
                small(v.tensor_tensor(cols[:, 34:35], gn_b, cols[:, 33:34], ALU.subtract))

                def residual0(m, s, g):
                    t = s % 8
                    if t % 4 == 0:
                        dve.wait_ge(xr_sems[t // 4], b * 256 + g * 32 + 32)
                    dve.wait_ge(gs_done, b * UNITS + m + 1)
                    xs = xring[:, t // 4, 512 * (t % 4):512 * (t % 4) + 512]
                    v.tensor_tensor(xs, xs, gring[:, s % 2, :], ALU.add).then_inc(x1_done, 1)
                    dve.wait_ge(x1_done, b * UNITS + m + 1)
                    v.bn_stats(stats[:, bass.ds(m, 1), :], xs).then_inc(st3_done, 1)

                bodies(dve, residual0, N0, 0, 8)
                dve.wait_ge(st3_done, b * UNITS + UNITS)
                group_norm(stats[:, :, :], 8, 5)
                v.tensor_copy(padrow[:, :], mean[0:64].to_broadcast([64, W])).then_inc(pad_done, 1)
                for k in range(2):
                    v.memset(ynorm[:, k, 0, 0:1, :], 0.0)
                    v.memset(ynorm[:, k, 0, W + 1:W + 2, :], 0.0)
                    v.memset(ynorm[0:64, k, 1, 0:1, :], 0.0)
                    v.memset(ynorm[0:64, k, 1, W + 1:W + 2, :], 0.0)
                    last = v.memset(ynorm[64:128, k, 1, W:W + 2, :], 0.0)
                last.then_inc(ln_ready, 1)

                def guard(n, t):
                    k = t % 2
                    dve.wait_ge(abs_done, b * NSB + n + 1)
                    v.tensor_scalar(mask, mask, THR, BIG, ALU.is_ge, ALU.mult).then_inc(mask_done, 1)
                    dve.wait_ge(mask_done, b * NSB + n + 1)
                    flat = "p a n -> p (a n)"
                    v.scalar_tensor_tensor(gspec.rearrange(flat), mask.rearrange(flat), THR,
                                           spec[:, k].rearrange(flat), ALU.add, ALU.max).then_inc(guard_done, 1)
                    dve.wait_ge(guard_done, b * NSB + n + 1)
                    v.tensor_tensor(prod[:, 0:2, :], gspec[:, 0:2, :], gspec[:, 2:4, :], ALU.mult)
                    v.tensor_tensor(prod[:, 2, :], gspec[:, 1, :], gspec[:, 2, :], ALU.mult)
                    v.tensor_tensor(prod[:, 3, :], gspec[:, 0, :], gspec[:, 3, :],
                                    ALU.mult).then_inc(sprod_done, 1)
                    dve.wait_ge(sprod_done, b * NSB + n + 1)
                    v.tensor_tensor(cross[:, 0, :], prod[:, 0, :], prod[:, 1, :], ALU.add)
                    v.tensor_tensor(cross[:, 1, :], prod[:, 2, :], prod[:, 3, :],
                                    ALU.subtract).then_inc(cross_done, 1)

                def spectra(n, t):
                    dve.wait_ge(rs_act, b * 3 * NSB + 3 * n + 3)
                    v.scalar_tensor_tensor(lnn[:, :, :], lnn[:, :, :], -0.5, n2[:, :, :],
                                           ALU.mult, ALU.mult).then_inc(rs_dve, 1)
                    dve.wait_ge(rs_dve, b * 2 * NSB + 2 * n + 1)
                    v.scalar_tensor_tensor(prod[:, :, :], lnn[:, :, :], 1.5, r0[:, :, :],
                                           ALU.add, ALU.mult).then_inc(rs_dve, 1)
                    dve.wait_ge(rs_dve, b * 2 * NSB + 2 * n + 2)
                    mags, amps = pmag[:, 0:3, :], pmag[:, 3:6, :]
                    v.tensor_tensor(mags[:, 0:2, :], n2[:, 2:4, :], prod[:, 2:4, :], ALU.mult)
                    v.tensor_tensor(mags[:, 2, :], prod[:, 0, :], prod[:, 1, :], ALU.mult).then_inc(mag_done, 1)
                    dve.wait_ge(mag_done, b * NSB + n + 1)
                    v.tensor_tensor(amps[:, 0:2, :], mags[:, 0:2, :],
                                    mags[:, 2, :].unsqueeze(1).to_broadcast([NF2, 2, SBN]), ALU.mult)
                    v.tensor_tensor(amps[:, 2, :], mags[:, 1, :], prod[:, 2, :], ALU.mult).then_inc(amp_done, 1)
                    dve.wait_ge(amp_done, b * NSB + n + 1)
                    dve.wait_ge(cross_done, b * NSB + n + 1)
                    if t >= 1:
                        dve.wait_ge(idft_done, b * 3 * NSB + 3 * n)
                    for j, (amp, z) in enumerate(((0, cross), (2, gspec[:, 4:6, :]), (1, cross))):
                        last = v.tensor_tensor(outs[:, 2 * j:2 * j + 2, :], z[:, 0:2, :],
                                               amps[:, amp, :].unsqueeze(1).to_broadcast([NF2, 2, SBN]), ALU.mult)
                    last.then_inc(outs_done, 1)

                def deviations(n, t):
                    for j in range(3):
                        dve.wait_ge(idft_done, b * 3 * NSB + 3 * n + (j + 1))
                        o = psum[:, 5 + (3 * t + j) % 2, 0:SBN].rearrange("p (b e) -> p b e", e=E)
                        v.tensor_reduce(lnst[:, 6, 4 * j:4 * j + 4], o, AX.X, ALU.add).then_inc(sum_done, 1)
                        dve.wait_ge(sum_done, b * 3 * NSB + 3 * n + (j + 1))
                        v.scalar_tensor_tensor(dev[:, j], bc(lnst[:, 6, 4 * j:4 * j + 4], E), -1.0 / E, o,
                                               ALU.mult, ALU.add).then_inc(dev_done, 1)

                def variances(n, t):
                    dve.wait_ge(dsq_done, b * 3 * NSB + 3 * n + 3)
                    v.tensor_reduce(lnst[:, 0, :], devsq.rearrange("p j b e -> p (j b) e"), AX.X,
                                    ALU.add).then_inc(var_done, 1)
                    dve.wait_ge(var_done, b * 2 * NSB + 2 * n + 1)
                    v.tensor_scalar(lnst[:, 1, :], lnst[:, 0, :], 1.0 / E, 1e-5, ALU.mult,
                                    ALU.add).then_inc(var_done, 1)
                    for j in range(3):
                        last = v.tensor_tensor(dev[:, j], dev[:, j], hdw[:, t % 4, :, 3 * E:E4], ALU.mult)
                    last.then_inc(vv_done, 1)

                def normalised(n, t):
                    dve.wait_ge(lr_act, b * 3 * NSB + 3 * n + 3)
                    v.scalar_tensor_tensor(lnst[:, 5, :], lnst[:, 4, :], -0.5, lnst[:, 1, :],
                                           ALU.mult, ALU.mult).then_inc(lr_dve, 1)
                    dve.wait_ge(lr_dve, b * 2 * NSB + 2 * n + 1)
                    v.scalar_tensor_tensor(lnst[:, 7, :], lnst[:, 5, :], 1.5, lnst[:, 3, :],
                                           ALU.add, ALU.mult).then_inc(lr_dve, 1)
                    dve.wait_ge(lr_dve, b * 2 * NSB + 2 * n + 2)
                    dve.wait_ge(vv_done, b * NSB + n + 1)
                    if t >= 2:
                        dve.wait_ge(proj_done, b * NSB + n - 1)
                    for j in range(3):
                        last = v.tensor_tensor(cat[:, t % 2, :, E * j:E * j + E], dev[:, j],
                                               bc(lnst[:, 7, 4 * j:4 * j + 4], E), ALU.mult)
                    last.then_inc(cat_done, 1)

                def residual1(n, t, loads_):
                    k = (t // SBROW) % 2
                    if t % SBROW == 0:
                        dve.wait_ge(os_sems[k], b * 256 + loads_ * 16)
                    dve.wait_ge(proj_done, b * NSB + n + 1)
                    c0 = 64 * (t % SBROW)
                    o = ostage[k][:, :, c0:c0 + 64]
                    v.tensor_tensor(o, o, psum[0:64, 7, :].rearrange("p (w r) -> p r w", r=P),
                                    ALU.add).then_inc(res_done, 1)

                def normalise_rows(row, t, g):
                    k = (t // SBROW) % 2
                    dve.wait_ge(xp_done, b * 64 * PROWS + row * 64 + 64)
                    if t >= 2 * SBROW:
                        dve.wait_ge(conv_done, b * 4 * NSB + row * 16 - 16)
                    for p0, p1, a, w0 in ((0, 128, 0, 1), (0, 64, 1, 1), (64, 128, 1, 0)):
                        last = v.tensor_scalar(ynorm[p0:p1, k, a, w0:w0 + W, :].rearrange("p w r -> p r w"),
                                               xraw[p0:p1, a], mean[p0:p1], rstd[p0:p1], ALU.subtract, ALU.mult)
                    last.then_inc(yp_done, 1)

                def layer1(m, s, g):
                    if s < NSB and s % SBROW == 0:
                        normalise_rows(m // SBROW if isinstance(m, int) else g * 2 + (s % LBODY) // SBROW, s, g)
                    if 2 <= s < NSB + 2:
                        deviations(m - 2, s - 2)
                    if 1 <= s < NSB + 1:
                        guard(m - 1, s - 1)
                    if 2 <= s < NSB + 2:
                        variances(m - 2, s - 2)
                    if s >= 4:
                        inside = isinstance(m, int)
                        residual1(m - 4, s - 4, (m - 4) // 8 + 1 if inside else g + (s % LBODY) // SBROW)
                    if 1 <= s < NSB + 1:
                        spectra(m - 1, s - 1)
                    if 2 <= s < NSB + 2:
                        normalised(m - 2, s - 2)

                bodies(dve, layer1, NSB, 4, LBODY)


def constants():
    import numpy as np
    f = np.float32
    p = np.arange(128)
    q, c = p // 64, p % 64
    diag = np.zeros((128, 130), f)
    diag[p, p] = 1
    diag[p, 128 + q] = 1 / 64
    avg2 = (c[:, None] // 2 == c[None] // 2).astype(f) / 4
    avg8 = (c[:, None] // 8 == c[None] // 8).astype(f) / 16
    avgq = (c[:, None] == c[None]).astype(f) / (H * W)
    swapq = ((p[:, None] + 64) % 128 == p[None]).astype(f)
    bands = np.zeros((128, 198), f)
    bands[p, p + K0 - BAND_LO] = 1
    r, col = p % P, p // P
    patch, cc = col // 8, col % 8
    ky, kx = np.arange(NF) // 5, np.arange(NF) % 5
    theta = 2 * np.pi * (r[:, None] * ky[None] + cc[:, None] * kx[None]) / P
    FR, FI = np.zeros((128, NF2)), np.zeros((128, NF2))
    GR, GI = np.zeros((NF2, 128)), np.zeros((NF2, 128))
    weight = np.where((kx == 0) | (kx == 4), 1.0, 2.0) / (P * P)
    for a in range(2):
        own = (patch == a)[:, None]
        FR[:, NF * a:NF * a + NF] = own * np.cos(theta)
        FI[:, NF * a:NF * a + NF] = own * -np.sin(theta)
        GR[NF * a:NF * a + NF] = (own * np.cos(theta) * weight).T
        GI[NF * a:NF * a + NF] = (own * -np.sin(theta) * weight).T
    return dict(consts=np.concatenate([diag, avg2, avg8, avgq, swapq], 1), bands=bands,
                FR=FR.astype(f), FI=FI.astype(f), GR=GR.astype(f), GI=GI.astype(f))


def kernel(**inputs):
    import numpy as np
    import concourse.bacc as bacc
    from concourse.bass_utils import run_bass_kernel_spmd as run

    g = {k: np.asarray(a) for k, a in inputs.items()}
    L0, L1 = "L0_conv_", "L1_conv_"
    col = lambda a: a.reshape(-1, 1)
    laid = dict(
        x=g["x"],
        w1T=g[L0 + "conv1_w"][:, :, 0, 0].T, conv1_b=col(g[L0 + "conv1_b"]),
        gn_g=col(g[L0 + "gn_g"]), gn_b=col(g[L0 + "gn_b"]), pw_b=col(g[L0 + "pw_b"]),
        pwT=g[L0 + "pw_w"].reshape(C, 3, C).transpose(2, 1, 0).reshape(C, 3 * C),
        dwc=np.concatenate([g[L0 + f"dw{k}_w"].reshape(C, -1) for k in (1, 2, 3)], 1),
        dbc=np.stack([g[L0 + f"dw{k}_b"] for k in (1, 2, 3)], 1),
        caw1T=g[L0 + "ca_w1"].reshape(8, C).T, caw2T=g[L0 + "ca_w2"].reshape(C, 8).T,
        sarow=np.concatenate([g[L0 + "sa_w"].reshape(1, 98), g[L0 + "sa_b"].reshape(1, 1)], 1),
        wdrow=g[L1 + "w_dw"].reshape(E4, 9).T.reshape(1, 9 * E4),
        whT=g[L1 + "w_hidden"].T,
        param=g[L1 + "fft_param"].reshape(E, NF).T,
        wpT=g[L1 + "w_proj"].reshape(C, 3, E).transpose(2, 1, 0).reshape(E, 3 * C),
        lnw=np.stack([g[L1 + f"ln{k}_w"] for k in (1, 2, 3)], 1),
        lnb=np.stack([g[L1 + f"ln{k}_b"] for k in (1, 2, 3)], 1),
        **constants(),
    )
    B = g["x"].shape[0]
    nc = bacc.Bacc("TRN2", target_bir_lowering=False, num_devices=1)
    arrays, io = {}, {}
    for name, a in laid.items():
        a = np.ascontiguousarray(a)
        arrays[f"in_{name}"] = a
        io[name] = nc.dram_tensor(f"in_{name}", a.shape, mybir.dt.from_np(a.dtype), kind="ExternalInput").ap()
    out = nc.dram_tensor("out_0", (B, C, H, W), F32, kind="ExternalOutput").ap()
    build(nc, B, io, out)
    r = run(nc, [arrays], core_ids=[0])
    return r.results[0]["out_0"]
```

```python
import concourse.bass as bass
from concourse import mybir
from concourse.alu_op_type import AluOpType as ALU
from contextlib import ExitStack

F32 = mybir.dt.float32
ACT = mybir.ActivationFunctionType
AX = mybir.AxisListType

C, H, W = 64, 256, 256
RP = H // 2
UNITS = RP // 2
BODY = 4
TAPS = 9
HR = 8
E = 76
E4 = 4 * E
P = 8
NF = P * (P // 2 + 1)
NF2 = 2 * NF
BLK = 4
SBN = BLK * E
NSB = (H // P) * (W // (16 * BLK))
PROWS = H // P
SBROW = NSB // PROWS
LBODY = 8
THR = 1e-10
BIG = -3.0e38
BAND_LO, BAND_N = 96, 192
K0 = 131
GN_EPS = 1e-5


def build(nc, B, io, out):
    ctx = ExitStack()
    with ctx:
        def sb(name, shape):
            return ctx.enter_context(nc.sbuf_tensor(name, shape, F32))

        def sem(name):
            return ctx.enter_context(nc.semaphore(name))

        x_in = io["x"]
        band7d = nc.dram_tensor("band7_scratch", (128, 14 * BAND_N), F32).ap()
        x1d = nc.dram_tensor("x1_scratch", (B, C, H + 2, W), F32).ap()

        WORK = 12612
        AREA = 46200
        arena = sb("arena", [128, AREA])
        img = arena[:, 0:RP * W].rearrange("p (r w) -> p r w", w=W)
        work = arena[:, RP * W:RP * W + WORK]
        K5 = sb("K5", [128, 2, 5, 128])
        PW5 = sb("PW5", [128, 128])
        tap_w = sb("tap_w", [128, TAPS])
        consts = sb("consts", [128, 130 + 4 * 128])
        diag130 = consts[:, 0:130]
        ident = consts[:, 0:128]
        avg2, avg8, avgq, swapq = (consts[:, 130 + 128 * k:258 + 128 * k] for k in range(4))
        ones_row = sb("ones_row", [1, 128])
        W1 = sb("W1", [128, 128])
        cols = sb("cols", [128, 64])
        b1 = cols[:, 0:1]
        cbias = cols[:, 1:2]
        gn_g, gn_b = cols[:, 2:3], cols[:, 3:4]
        sa_b = cols[:, 4:5]
        pwb = cols[:, 5:6]
        half_ln = cols[:, 6:7]
        caw1 = sb("caw1", [128, 8])
        caw2 = sb("caw2", [8, 128])
        saw = sb("saw", [128, 99])
        stats = sb("stats", [128, UNITS, 6])
        mxs = sb("mxs", [128, UNITS])
        sms = sb("sms", [128, UNITS])
        WA = sb("WA", [128, 3, E4])
        WB = sb("WB", [128, 2, E4])
        param = sb("param", [NF2, E])
        WP = sb("WP", [128, 3, C])
        FR = sb("FR", [128, NF2])
        FI = sb("FI", [128, NF2])
        GR = sb("GR", [NF2, 128])
        GI = sb("GI", [NF2, 128])

        hring = work[:, 0:HR * 260].rearrange("p (r w) -> p r w", w=260)
        yring = work[:, 2080:2080 + 4 * 512].rearrange("p (k n) -> p k n", k=4)
        zring = work[:, 4128:4128 + 2 * 512].rearrange("p (k n) -> p k n", k=2)
        near = work[:, 5300:5300 + HR * 260].rearrange("p (r w) -> p r w", w=260)
        far = work[:, 7400:7400 + HR * 260].rearrange("p (r w) -> p r w", w=260)
        swap = work[:, 10532:10532 + HR * 260].rearrange("p (r w) -> p r w", w=260)
        tapsum = work[:, 9500:9500 + 2 * 512].rearrange("p (k n) -> p k n", k=2)
        cring = work[:, 0:2 * 512].rearrange("p (k n) -> p k n", k=2)
        saring = work[:, 2600:2600 + 2 * 512].rearrange("p (k h r c) -> p k h r c", k=2, h=2, r=4)
        saca = work[:, 0:2 * 512].rearrange("p (k n) -> p k n", k=2)
        band7 = work[:, 2600:2600 + 14 * BAND_N].rearrange("p (n u) -> p n u", n=14)
        maps = work[:, 1040:1040 + 4 * (H + 6)].rearrange("p (a h r) -> p a h r", a=2, h=2)
        sa = work[:, 2088:2088 + 2 * H].rearrange("p (h r) -> p h r", h=2)
        xring = work[:, 1600:1600 + 4 * 2048].rearrange("p (k n) -> p k n", k=4)
        gring = work[:, 9792:9792 + 4 * 512].rearrange("p (k n) -> p k n", k=4)
        padrow = sb("padrow", [64, W])

        used = [0]

        def carve(parts, n):
            a = arena[0:parts, used[0]:used[0] + n]
            used[0] += n
            return a

        xraw = carve(128, 2 * P * W).rearrange("p (a r w) -> p a r w", a=2, w=W)
        ynorm = carve(128, 2 * 2 * (W + 2) * P).rearrange("p (k a w r) -> p k a w r", k=2, a=2, r=P)
        stage = carve(128, P * W).rearrange("p (r w) -> p r w", w=W)
        ostage = (stage[0:64], stage[64:128])
        hdw = carve(128, 4 * BLK * E4).rearrange("p (k b n) -> p k b n", k=4, b=BLK)
        spec = carve(NF2, 2 * 8 * SBN).rearrange("p (k a n) -> p k a n", k=2, a=8)
        mask = carve(NF2, 8 * SBN).rearrange("p (a n) -> p a n", a=8)
        gspec = carve(NF2, 6 * SBN).rearrange("p (a n) -> p a n", a=6)
        gv = carve(NF2, 2 * 2 * SBN).rearrange("p (k a n) -> p k a n", k=2, a=2)
        prod = carve(NF2, 4 * SBN).rearrange("p (a n) -> p a n", a=4)
        pprod = carve(NF2, 4 * SBN).rearrange("p (a n) -> p a n", a=4)
        cross = carve(NF2, 2 * 2 * SBN).rearrange("p (k a n) -> p k a n", k=2, a=2)
        n2 = carve(NF2, 4 * SBN).rearrange("p (a n) -> p a n", a=4)
        lnn = carve(NF2, 4 * SBN).rearrange("p (a n) -> p a n", a=4)
        r0 = carve(NF2, 4 * SBN).rearrange("p (a n) -> p a n", a=4)
        roots, mags, amps = r0, lnn[:, 0:3, :], r0[:, 0:3, :]
        outs = carve(NF2, 6 * SBN).rearrange("p (a n) -> p a n", a=6)
        dev = carve(128, 2 * 3 * SBN).rearrange("p (k j b e) -> p k j b e", k=2, j=3, e=E)
        devsq = carve(128, 3 * SBN).rearrange("p (j b e) -> p j b e", j=3, e=E)
        cat = carve(128, 2 * BLK * E4).rearrange("p (k b n) -> p k b n", k=2, b=BLK)
        catT = carve(128, 3 * 512).rearrange("p (a n) -> p a n", a=3)
        lnst = carve(128, 8 * 12).rearrange("p (k n) -> p k n", k=8)
        assert used[0] <= AREA and RP * W + WORK <= AREA, used[0]
        used[0] = 0
        band7_new = carve(128, 14 * BAND_N).rearrange("p (n u) -> p n u", n=14)
        dense5 = carve(128, 25 * C).rearrange("p (t n) -> p t n", n=C)
        pwT = carve(128, 3 * C).rearrange("p (j n) -> p j n", j=3)
        dwc = carve(128, 35)
        dbc = carve(128, 3)
        bands = carve(128, 198)
        sarow = carve(1, 99)
        wdrow = carve(1, 9 * E4)
        wdb = carve(128, 9 * E4).rearrange("p (t n) -> p t n", t=9)
        whT = carve(128, E4)
        wp4 = carve(E, 4 * C).rearrange("p (j n) -> p j n", j=4)
        wpr = carve(E, 3 * C).rearrange("p (j n) -> p j n", j=3)
        lnw = carve(E, 3)
        lnb = carve(E, 3)

        psum = ctx.enter_context(nc.psum_tensor("psum", [128, 8, 512], F32))

        def bank(k):
            return psum[:, k, :]

        loaded = sem("setup_loaded")
        memset_done = sem("memset_done")
        v_setup = sem("v_setup")
        p_setup = sem("p_setup")
        wp4_done = sem("wp4_done")
        setup_done = sem("setup_done")
        band_stored = sem("band_stored")
        band_loaded = sem("band_loaded")
        packed = sem("packed")
        image_done = sem("image_done")
        x_in_sems = [sem(f"x_loaded{k}") for k in range(4)]
        stat_done = sem("x_stats")
        gn = sem("gn_small")
        gmm = sem("gn_matmul")
        gact = sem("gn_act")
        y_done = sem("y_done")
        c1_done = sem("conv1_done")
        h_done = sem("h_done")
        taps_done = sem("depthwise_taps")
        edge_done = sem("zeros_below")
        c5_done = sem("conv5_done")
        z_done = sem("z_done")
        zs_done = sem("z_plus_y")
        img_done = sem("h_image")
        red_done = sem("h_reduced")
        cp_done = sem("scaled_copy")
        tr_done = sem("transposed")
        map_done = sem("maps_done")
        sac_done = sem("sa_conv")
        sa_done = sem("sa_done")
        sar_done = sem("sa_rows")
        sab_done = sem("sa_broadcast")
        saca_done = sem("sa_ca_odd")
        out2_done = (sem("sa_ca_h_even"), sem("sa_ca_h_odd"))
        st2_done = sem("out_stats")
        xr_sems = [sem(f"x_again{k}") for k in range(4)]
        gs_done = sem("gn_silu")
        x1_done = (sem("x1_even"), sem("x1_odd"))
        st3_done = sem("x1_stats")
        x1_stored = [sem(f"x1_stored{k}") for k in range(4)]
        pad_done = sem("pad_row")
        pad_stored = sem("pad_stored")
        ln_ready = sem("layer1_ready")
        xp_done = sem("patch_rows_loaded")
        yp_done = sem("patch_rows_normalised")
        conv_done = sem("conv_done")
        hdw_done = sem("hdw_evacuated")
        dft_done = sem("dft_done")
        ft_done = sem("dft_evacuated")
        vpar_done = sem("v_times_param")
        qkp_done = sem("qk_products")
        qk_done = sem("qk_done")
        abs_done = sem("abs_all")
        mask_done = sem("guard_mask")
        guard_done = sem("guarded")
        sprod_done = sem("cross_products")
        cross_done = sem("cross_done")
        sq_done = sem("squares_done")
        n2_done = sem("norms2_done")
        rs_act = sem("rsqrt_act")
        rs_dve = sem("rsqrt_newton")
        mag_done = sem("magnitudes")
        amp_done = sem("amplitudes")
        outs_done = sem("outs_done")
        idft_done = sem("idft_done")
        sum_done = sem("ln_sum")
        dev_done = sem("ln_dev")
        dsq_done = sem("ln_devsq")
        var_done = sem("ln_var")
        vv_done = sem("ln_dev_vv")
        lr_act = sem("ln_rstd_act")
        lr_dve = sem("ln_rstd_newton")
        vcp_done = sem("vv_in_cat")
        cat_done = sem("cat_done")
        proj_done = sem("proj_done")
        os_sems = [sem(f"residual_loaded{k}") for k in range(2)]
        res_done = sem("residual_added")
        st_sems = [sem(f"out_stored{k}") for k in range(2)]

        block = ctx.enter_context(nc.Block())

        def unit(t):
            return img[:, bass.ds(2 * t, 2), :]

        def pairs(a):
            return a.rearrange("p (r w) -> p r w", w=W)

        def bc(a, n):
            return a.unsqueeze(len(a.shape)).to_broadcast(list(a.shape) + [n])

        def bodies(eng, step, n_steps, lag, size, last=0, peel=8):
            for m in range(peel):
                step(m, m, m // size)
            with eng.Fori(peel // size, (n_steps - last) // size) as i:
                for u in range(size):
                    step(i * size + u, peel + u, i)
            for m in range(n_steps - last, n_steps + lag):
                step(m, m, m // size)

        def pair_of(m, s, g, size):
            return m // 2 if isinstance(m, int) else g * (size // 2) + s % size // 2

        N0 = UNITS
        N_CHUNKS = RP // 8
        USES = 9 * NSB
        G_V, G_A, G_M = 26, 5, 10
        rows3 = (128, 128, E4 - 256)

        def tuse(m, s, k):
            return 9 * m - 12 + k if s < NSB else 9 * NSB - 12 + 3 * (m - NSB) + k

        def use(m, s, k):
            return 6 * m + k if s < 4 else 9 * m - 9 + k

        loads = [
            (consts[:, :], io["consts"]), (bands, io["bands"]),
            (FR[:, :], io["FR"]), (FI[:, :], io["FI"]), (GR[:, :], io["GR"]), (GI[:, :], io["GI"]),
            (b1[0:64], io["conv1_b"]), (b1[64:128], io["conv1_b"]),
            (gn_g[0:64], io["gn_g"]), (gn_g[64:128], io["gn_g"]),
            (gn_b[0:64], io["gn_b"]), (gn_b[64:128], io["gn_b"]),
            (pwb[0:64], io["pw_b"]), (pwb[64:128], io["pw_b"]),
            (pwT[0:64], io["pwT"]), (pwT[64:128], io["pwT"]),
            (dwc[0:64], io["dwc"]), (dwc[64:128], io["dwc"]),
            (dbc[0:64], io["dbc"]),
            (caw1[0:64, :], io["caw1T"]), (caw2[:, 0:64], io["caw2T"]), (caw2[:, 64:128], io["caw2T"]),
            (sarow, io["sarow"]), (wdrow, io["wdrow"]),
            (whT[0:64], io["whT"]), (whT[64:128], io["whT"]),
            (param[0:NF, :], io["param"]), (param[NF:NF2, :], io["param"]),
            (wpr, io["wpT"]), (lnw, io["lnw"]), (lnb, io["lnb"]),
            (W1[0:64, 0:64], io["w1T"]), (W1[64:128, 64:128], io["w1T"]),
        ]
        packs = []
        for a_ in range(4):
            done_ = 0
            while done_ < E:
                row_ = a_ * E + done_
                n_ = min(E - done_, 128 - row_ % 128)
                packs.append((WP[row_ % 128:row_ % 128 + n_, row_ // 128, :], wp4[done_:done_ + n_, a_, :]))
                done_ += n_

        @block.sync
        def _(sp):
            sp.wait_ge(memset_done, 1)
            for dst, src in loads:
                sp.dma_start(dst, src).then_inc(loaded, 16)
            sp.wait_ge(wp4_done, 1)
            for dst, src in packs:
                sp.dma_start(dst, src).then_inc(packed, 16)
            sp.wait_ge(setup_done, 1)
            sp.dma_start(band7d, band7_new.rearrange("p n u -> p (n u)")).then_inc(band_stored, 16)
            sp.wait_ge(band_stored, 16)
            sp.wait_ge(packed, 16 * len(packs))
            sp.sem_inc(image_done, 1)
            with sp.Fori(0, B) as b:
                sp.wait_ge(image_done, b + 1)
                xv = x_in[bass.ds(b, 1)].rearrange("o c (i q) w -> (o q) c i w", q=2)

                def load_x(i):
                    for k in range(4):
                        for q in range(2):
                            sp.dma_start(img[64 * q:64 * q + 64, bass.ds(i * 32 + 8 * k, 8), :],
                                         xv[q, :, bass.ds(i * 32 + 8 * k, 8), :]).then_inc(x_in_sems[k], 16)

                load_x(0)
                with sp.Fori(1, N_CHUNKS // 4) as i:
                    sp.wait_ge(stat_done, b * UNITS + i * 16)
                    load_x(i)

                sp.wait_ge(red_done, b * UNITS + UNITS)
                sp.dma_start(band7.rearrange("p n u -> p (n u)"), band7d).then_inc(band_loaded, 16)

                x1v = x1d[bass.ds(b, 1), :, 1:H + 1, :].rearrange("o c (i q) w -> (o q) c i w", q=2)

                def load_again(j, k):
                    for q in range(2):
                        sp.dma_start(pairs(xring[64 * q:64 * q + 64, k, :]),
                                     xv[q, :, bass.ds(j * 8, 8), :]).then_inc(xr_sems[k], 16)

                def store_x1(j, k):
                    for par in range(2):
                        sp.wait_ge(x1_done[par], b * (UNITS // 2) + j * 2 + 2)
                    for q in range(2):
                        sp.dma_start(x1v[q, :, bass.ds(j * 8, 8), :],
                                     pairs(xring[64 * q:64 * q + 64, k, :])).then_inc(x1_stored[k], 16)

                sp.wait_ge(sac_done, b + 1)
                for j in range(3):
                    load_again(j, j + 1)
                for par in range(2):
                    sp.wait_ge(out2_done[par], b * (UNITS // 2) + UNITS // 2)
                load_again(3, 0)
                with sp.Fori(0, N_CHUNKS // 4 - 1) as i:
                    for j in range(4):
                        k = (j + 1) % 4
                        store_x1(i * 4 + j, k)
                        sp.wait_ge(st3_done, b * UNITS + i * 16 + (4 * j + 4))
                        sp.wait_ge(x1_stored[k], b * 128 + i * 32 + 32)
                        load_again(i * 4 + (j + 4), k)
                for j in range(4):
                    store_x1(N_CHUNKS - 4 + j, (j + 1) % 4)
                sp.wait_ge(pad_done, b + 1)
                for k in range(4):
                    sp.wait_ge(x1_stored[k], b * 128 + 128)
                for r in (H + 1, 0):
                    sp.dma_start(x1d[bass.ds(b, 1), :, r:r + 1, :].rearrange("o c r w -> (o c) (r w)"),
                                 padrow[:, :]).then_inc(pad_stored, 16)
                sp.wait_ge(pad_stored, b * 32 + 32)
                sp.wait_ge(ln_ready, b + 1)
                sv = x1d[bass.ds(b, 1)].rearrange("o c r w -> (o c) r w")
                ov = out[bass.ds(b, 1)].rearrange("o c r w -> (o c) r w")

                def load_rows(j):
                    for half, a, dy in ((0, 0, 0), (1, 0, 1), (0, 1, 2), (1, 1, 2)):
                        sp.dma_start(xraw[64 * half:64 * half + 64, a],
                                     sv[:, bass.ds(j * 8 + dy, 8), :]).then_inc(xp_done, 16)

                def store_rows(j, k):
                    sp.wait_ge(res_done, b * NSB + j * SBROW + SBROW)
                    sp.dma_start(ov[:, bass.ds(j * 8, 8), :], ostage[k]).then_inc(st_sems[k], 16)

                def load_residual(j, k):
                    sp.dma_start(ostage[k], sv[:, bass.ds(j * 8 + 1, 8), :]).then_inc(os_sems[k], 16)

                load_rows(0)
                for k in range(2):
                    load_residual(k, k)
                sp.wait_ge(yp_done, b * PROWS + 1)
                load_rows(1)
                with sp.Fori(1, PROWS // 2) as i:
                    for k in range(2):
                        sp.wait_ge(yp_done, b * PROWS + i * 2 + k)
                        load_rows(i * 2 + k)
                        store_rows(i * 2 + (k - 2), k)
                        sp.wait_ge(st_sems[k], b * 256 + i * 16)
                        load_residual(i * 2 + k, k)
                for k in range(2):
                    store_rows(PROWS - 2 + k, k)
                for k in range(2):
                    sp.wait_ge(st_sems[k], b * 256 + 256)
                sp.sem_inc(image_done, 1)

        @block.tensor
        def _(pe):
            mm = nc.tensor.matmul
            pe.wait_ge(loaded, 16 * len(loads))
            pe.wait_ge(memset_done, 2)
            for q in range(2):
                for j in range(3):
                    last = mm(psum[64 * q:64 * q + 64, 0, 0:1], pwT[0:64, j, :], dbc[0:64, j:j + 1],
                              start=(j == 0), stop=(j == 2))
            last.then_inc(p_setup, 1)
            mm(psum[:, 1, 0:99], ones_row[:, :], sarow, start=True, stop=True).then_inc(p_setup, 1)
            for k in range(6):
                mm(psum[:, 2 + k, 0:456], ones_row[:, :], wdrow[:, 456 * k:456 * k + 456],
                   start=True, stop=True).then_inc(p_setup, 1)
            pe.wait_ge(setup_done, 1)
            pe.wait_ge(packed, 16 * len(packs))

            with pe.Fori(0, B) as b:
                pe.wait_ge(image_done, b + 1)

                def stat(matrix, rhs, need):
                    pe.wait_ge(gn, b * G_V + need)
                    mm(psum[:, 7, 0:1], matrix, rhs, start=True, stop=True).then_inc(gmm, 1)

                mean_col, var_col = cols[:, 16:17], cols[:, 20:21]
                stat(avg2, mean_col, 1)
                stat(avg2, var_col, 4)

                def convs(m, s, g):
                    if s < N0:
                        pe.wait_ge(y_done, b * UNITS + m + 1)
                        if s >= 2:
                            pe.wait_ge(h_done, b * UNITS + m - 1)
                        mm(bank(s % 2), W1[:, :], yring[:, s % 4, :], start=True, stop=True).then_inc(c1_done, 1)
                    t = s - 2
                    if t < 0:
                        return
                    pe.wait_ge(h_done, b * UNITS + (m if t < N0 - 1 else m - 1))
                    if t >= 2:
                        pe.wait_ge(z_done, b * UNITS + m - 3)
                    if t == N0 - 1:
                        pe.wait_ge(edge_done, b + 1)
                    o = psum[:, 2 + t % 2, :]
                    at, above = (2 * t) % HR, (2 * t + 1) % HR
                    for dx in (1, 2, 3):
                        mm(o, K5[:, 0, dx, :], hring[:, at:at + 2, dx:dx + W], start=(dx == 1), stop=False)
                    for dx in range(5):
                        if above < HR - 1:
                            mm(o, K5[:, 1, dx, :], near[:, above:above + 2, dx:dx + W], start=False, stop=False)
                        else:
                            for r, place in ((0, HR - 1), (1, 0)):
                                mm(o[:, 256 * r:256 * r + 256], K5[:, 1, dx, :], near[:, place, dx:dx + W],
                                   start=False, stop=False, skip_group_check=True)
                    pe.wait_ge(taps_done, b * TAPS * UNITS + TAPS * m - TAPS)
                    mm(o, PW5[:, :], tapsum[:, t % 2, :], start=False, stop=True).then_inc(c5_done, 1)

                bodies(pe, convs, N0, 2, BODY)

                stat(avgq, cols[:, 24:25], 8)
                stat(swapq, cols[:, 25:26], 9)
                pe.wait_ge(gn, b * G_V + 10)
                mm(psum[0:8, 7, 0:2], caw1[:, :], cols[:, 26:28], start=True, stop=True).then_inc(gmm, 1)
                pe.wait_ge(gact, b * G_A + 2)
                mm(psum[:, 7, 0:2], caw2[:, :], cols[0:8, 28:30], start=True, stop=True).then_inc(gmm, 1)

                def transposes(m, s, g):
                    pe.wait_ge(cp_done, b * UNITS + m + 1)
                    if s >= 2:
                        pe.wait_ge(map_done, b * UNITS + m - 1)
                    for r in range(2):
                        for hf in range(2):
                            last = mm(psum[:, 2 * (s % 2) + r, 130 * hf:130 * hf + 130],
                                      cring[:, s % 2, 256 * r + 128 * hf:256 * r + 128 * hf + 128],
                                      diag130, start=True, stop=True)
                    last.then_inc(tr_done, 1)

                bodies(pe, transposes, N0, 0, BODY)

                pe.wait_ge(map_done, b * UNITS + UNITS)
                pe.wait_ge(band_loaded, b * 16 + 16)
                for ho in range(2):
                    hi = 1 - ho
                    p0, u0 = (96, 96) if hi == 1 else (0, 256)
                    for n in range(14):
                        a, dy = n // 7, n % 7
                        mm(psum[:, 4, 256 * ho:256 * ho + 256], band7[:, n, 128 - BAND_LO:256 - BAND_LO],
                           maps[:, a, ho, dy:dy + H], start=(n == 0), stop=(n == 13))
                    for n in range(14):
                        a, dy = n // 7, n % 7
                        last = mm(psum[p0:p0 + 32, 4, 256 * ho:256 * ho + 256],
                                  band7[:, n, u0 - BAND_LO:u0 + 32 - BAND_LO],
                                  maps[:, a, hi, dy:dy + H], start=False, stop=(n == 13), skip_group_check=True)
                last.then_inc(sac_done, 1)

                def spread(m, s, g):
                    pe.wait_ge(sar_done, b * UNITS + m + 1)
                    if s >= 4:
                        pe.wait_ge((out2_done[0], saca_done)[s % 2], b * (UNITS // 2) + pair_of(m, s, g, BODY) - 1)
                    for r in range(2):
                        for hf in range(2):
                            last = nc.tensor.transpose(
                                psum[:, s % 4, 256 * r + 128 * hf:256 * r + 128 * hf + 128],
                                saring[:, s % 2, hf, 2 * r:2 * r + 2, :].rearrange("p q c -> p (q c)"), ident)
                    last.then_inc(sab_done, 1)

                bodies(pe, spread, N0, 0, BODY)
                stat(avg8, mean_col, 12)
                stat(avg8, var_col, 15)
                stat(avg2, mean_col, 21)
                stat(avg2, var_col, 24)

                pe.wait_ge(ln_ready, b + 1)

                def idft(n, t):
                    pe.wait_ge(outs_done, b * NSB + n + 1)
                    for j in range(3):
                        if t >= 1:
                            pe.wait_ge(dev_done, b * 3 * NSB + 3 * n + (j - 2))
                        o = psum[:, 5 + j, 0:SBN]
                        mm(o, GR[:, :], outs[:, 2 * j, :], start=True, stop=False)
                        mm(o, GI[:, :], outs[:, 2 * j + 1, :], start=False, stop=True).then_inc(idft_done, 1)

                def conv(n, t, row):
                    k = (t // SBROW) % 2
                    if t % SBROW == 0:
                        pe.wait_ge(yp_done, b * PROWS + row + 1)
                    for q in range(BLK):
                        if 4 * t + q >= 2:
                            pe.wait_ge(hdw_done, b * 4 * NSB + 4 * n + (q - 1))
                        c0 = 64 * (t % SBROW) + 16 * q
                        o = psum[:, q % 2, 0:E4]

                        def pixels(half, a, dx):
                            return ynorm[0:64 * half, k, a, c0 + dx:c0 + dx + 16, :].rearrange("p w r -> p (w r)")

                        for dx in range(3):
                            mm(o, pixels(2, 0, dx), WA[:, dx, :], start=(dx == 0), stop=False)
                        mm(o, pixels(2, 1, 0), WB[:, 0, :], start=False, stop=False)
                        mm(o, pixels(1, 1, 2), WB[0:64, 1, :], start=False, stop=True).then_inc(conv_done, 1)

                def dft(n, t):
                    pe.wait_ge(hdw_done, b * 4 * NSB + 4 * n + 4)
                    for k in range(6):
                        if 6 * t + k >= 3:
                            pe.wait_ge(ft_done, b * USES + use(n, t, k) - 2)
                        mm(psum[0:NF2, 2 + k % 3, 0:SBN], (FR, FI)[k % 2][:, :],
                           hdw[:, t % 4, :, (k // 2) * E:(k // 2) * E + E],
                           start=True, stop=True).then_inc(dft_done, 1)

                def transpose_cat(n, t, m, s):
                    pe.wait_ge(cat_done, b * NSB + n + 1)
                    pe.wait_ge(vcp_done, b * NSB + n + 1)
                    if t >= 1:
                        pe.wait_ge(res_done, b * NSB + n)
                    pe.wait_ge(ft_done, b * USES + tuse(m, s, 2) - 2)
                    for k, rows in enumerate(rows3):
                        for q in range(BLK):
                            last = nc.tensor.transpose(psum[0:rows, 2 + k, 128 * q:128 * q + 128],
                                                       cat[:, t % 2, q, 128 * k:128 * k + rows], ident)
                        last.then_inc(dft_done, 1)

                def project(n, t, m, s):
                    pe.wait_ge(ft_done, b * USES + (use(m, s, 3) if s < NSB else tuse(m, s, 2)) + 1)
                    for k, rows in enumerate(rows3):
                        last = mm(psum[0:64, 2, :], WP[0:rows, k, :], catT[0:rows, k, :],
                                  start=(k == 0), stop=(k == 2))
                    last.then_inc(proj_done, 1)

                def layer1(m, s, g):
                    if 3 <= s < NSB + 3:
                        idft(m - 3, s - 3)
                    if s < NSB:
                        conv(m, s, m // SBROW if isinstance(m, int) else g * 2 + (s % LBODY) // SBROW)
                    if s >= 4:
                        transpose_cat(m - 4, s - 4, m, s)
                    if s < NSB:
                        dft(m, s)
                    if s >= 4:
                        project(m - 4, s - 4, m, s)

                bodies(pe, layer1, NSB, 4, LBODY)

        @block.scalar
        def _(act):
            fn = nc.scalar.activation
            with act.Fori(0, B) as b:
                act.wait_ge(image_done, b + 1)

                def root(k, need):
                    act.wait_ge(gn, b * G_V + need)
                    fn(cols[:, 22:23], cols[:, 21:22], ACT.Sqrt).then_inc(gact, 1)

                root(1, 5)

                def silus(m, s, g):
                    if s < N0:
                        act.wait_ge(c1_done, b * UNITS + m + 1)
                        if s >= 4:
                            act.wait_ge(c5_done, b * UNITS + m - 2)
                            act.wait_ge(taps_done, b * TAPS * UNITS + TAPS * m - 2 * TAPS)
                        c1 = pairs(bank(s % 2))

                        def put(ring, q, at, to=None):
                            to = q if to is None else to
                            for r0_, n in ((0, 2),) if at % HR < HR - 1 else ((0, 1), (1, 1)):
                                slot = (at + r0_) % HR
                                half = slice(64 * q, 64 * q + 64)
                                i = fn(ring[64 * to:64 * to + 64, slot:slot + n, 2:2 + W], c1[half, r0_:r0_ + n, :],
                                       ACT.Silu, bias=b1[half])
                            return i

                        r = (2 * s) % HR
                        fn(hring[:, r:r + 2, 2:2 + W], c1, ACT.Silu, bias=b1)
                        put(swap, 0, 2 * s, 1)
                        put(swap, 1, 2 * s, 0)
                        put(near, 0, 2 * s)
                        put(near, 1, 2 * s + 2)
                        if s > 0:
                            put(far, 1, 2 * s - 1)
                        else:
                            fn(far[64:128, 0:1, 2:2 + W], c1[64:128, 1:2, :], ACT.Silu, bias=b1[64:128])
                        put(far, 0, 2 * s + 1).then_inc(h_done, 1)
                    if 3 <= s < N0 + 3:
                        t = s - 3
                        act.wait_ge(c5_done, b * UNITS + m - 2)
                        if t >= 2:
                            act.wait_ge(img_done, b * UNITS + m - 4)
                        fn(zring[:, t % 2, :], bank(2 + t % 2), ACT.Silu, bias=cbias).then_inc(z_done, 1)
                    if s >= 4:
                        act.wait_ge(zs_done, b * UNITS + m - 3)
                        fn(unit(m - 4), pairs(zring[:, (s - 4) % 2, :]), ACT.Silu).then_inc(img_done, 1)

                bodies(act, silus, N0, 4, BODY)

                act.wait_ge(gmm, b * G_M + 5)
                fn(cols[0:8, 28:30], psum[0:8, 7, 0:2], ACT.Relu).then_inc(gact, 1)
                act.wait_ge(gn, b * G_V + 11)
                ca = cols[:, 31:32]
                fn(ca, cols[:, 30:31], ACT.Silu).then_inc(gact, 1)
                act.wait_ge(gact, b * G_A + 3)

                def scaled(m, s, g):
                    if s >= 2:
                        act.wait_ge(tr_done, b * UNITS + m - 1)
                    fn(pairs(cring[:, s % 2, :]), unit(m), ACT.Copy, scale=ca).then_inc(cp_done, 1)

                bodies(act, scaled, N0, 0, BODY)

                act.wait_ge(sac_done, b + 1)
                fn(sa[:, :, :], psum[:, 4, :].rearrange("p (h n) -> p h n", h=2), ACT.Silu,
                   bias=sa_b).then_inc(sa_done, 1)

                act.wait_ge(sa_done, b + 1)

                def sa_rows(m, s, g):
                    if s < N0:
                        if s >= 2:
                            act.wait_ge(sab_done, b * UNITS + m - 1)
                        fn(saring[:, s % 2],
                           bc(sa[:, :, bass.ds(m * 4, 4)], 64), ACT.Copy).then_inc(sar_done, 1)
                    if s >= 2 and s % 2 == 0:
                        act.wait_ge(sab_done, b * UNITS + m)
                        if s >= 6:
                            act.wait_ge(out2_done[1], b * (UNITS // 2) + pair_of(m, s, g, BODY) - 2)
                        fn(saca[:, (s // 2 - 1) % 2, :], bank((s - 1) % 4), ACT.Copy, scale=ca).then_inc(saca_done, 1)

                bodies(act, sa_rows, N0, 1, BODY)

                root(4, 16)
                act.wait_ge(gn, b * G_V + 20)

                def gn_silu(m, s, g):
                    if s >= 4:
                        act.wait_ge(x1_done[s % 2], b * (UNITS // 2) + pair_of(m, s, g, BODY) - 1)
                    fn(pairs(gring[:, s % 4, :]), unit(m), ACT.Silu, bias=cols[:, 34:35],
                       scale=cols[:, 32:33]).then_inc(gs_done, 1)

                bodies(act, gn_silu, N0, 0, BODY)
                root(5, 25)

                act.wait_ge(ln_ready, b + 1)

                def evacuate(n, t, q):
                    act.wait_ge(conv_done, b * 4 * NSB + 4 * n + (q + 1))
                    if t >= 4 and q == 0:
                        act.wait_ge(vv_done, b * NSB + n - 3)
                        act.wait_ge(vcp_done, b * NSB + n - 3)
                    fn(hdw[:, t % 4, q, :], psum[:, q % 2, 0:E4], ACT.Copy).then_inc(hdw_done, 1)

                def layer1(m, s, g):
                    n, t, k = m - 1, s - 1, (s - 1) % 2
                    new, old = 0 <= t < NSB, 3 <= s < NSB + 3
                    rbase, lbase = b * 3 * NSB + 3 * n, b * 3 * NSB + 3 * m - 9
                    if new:
                        act.wait_ge(vpar_done, b * NSB + n + 1)
                        act.wait_ge(qk_done, b * NSB + n + 1)
                        if t >= 1:
                            act.wait_ge(n2_done, b * NSB + n)
                        fn(mask, spec[:, k], ACT.Abs).then_inc(abs_done, 1)
                    if s < NSB:
                        evacuate(m, s, 0)
                    if old:
                        if s >= 5:
                            act.wait_ge(proj_done, b * NSB + m - 4)
                        fn(cat[:, (s - 3) % 2, :, 3 * E:E4], hdw[:, (s - 3) % 4, :, 3 * E:E4],
                           ACT.Copy).then_inc(vcp_done, 1)
                    if s < NSB:
                        evacuate(m, s, 1)
                    if old:
                        for j in range(3):
                            act.wait_ge(dev_done, lbase + (j + 1))
                            if s >= 4 and j == 0:
                                act.wait_ge(var_done, b * 2 * NSB + 2 * m - 7)
                            fn(devsq[:, j], dev[:, (s - 3) % 2, j], ACT.Square).then_inc(dsq_done, 1)
                    if s < NSB:
                        evacuate(m, s, 2)
                    if new:
                        act.wait_ge(guard_done, b * NSB + n + 1)
                        fn(mask[:, 0:6, :], gspec, ACT.Square)
                        fn(mask[:, 6:8, :], gv[:, k], ACT.Square).then_inc(sq_done, 1)
                    if s < NSB:
                        evacuate(m, s, 3)
                    if s >= 4:
                        for c, rows in enumerate(rows3):
                            act.wait_ge(dft_done, b * USES + tuse(m, s, c) + 1)
                            if s >= 5 and c == 0:
                                act.wait_ge(proj_done, b * NSB + m - 4)
                            fn(catT[0:rows, c, :], psum[0:rows, 2 + c, :], ACT.Copy).then_inc(ft_done, 1)
                    if s < NSB:
                        if s >= 2:
                            act.wait_ge(guard_done, b * NSB + m - 1)
                        for c in range(6):
                            act.wait_ge(dft_done, b * USES + use(m, s, c) + 1)
                            fn(spec[:, s % 2, (0, 1, 2, 3, 6, 7)[c], :], psum[0:NF2, 2 + c % 3, 0:SBN],
                               ACT.Copy).then_inc(ft_done, 1)
                    if new:
                        act.wait_ge(n2_done, b * NSB + n + 1)
                        if t >= 1:
                            act.wait_ge(amp_done, b * NSB + n)
                        fn(lnn[:, :, :], n2[:, :, :], ACT.Ln, scale=65536.0).then_inc(rs_act, 1)
                    if old:
                        act.wait_ge(var_done, b * 2 * NSB + 2 * m - 4)
                        if s >= 4:
                            act.wait_ge(lr_dve, b * 2 * NSB + 2 * m - 6)
                        fn(lnst[:, 2, :], lnst[:, 1, :], ACT.Ln).then_inc(lr_act, 1)
                    if old:
                        act.wait_ge(lr_act, lbase + 1)
                        fn(lnst[:, 3, :], lnst[:, 2, :], ACT.Exp, scale=-0.5).then_inc(lr_act, 1)
                        act.wait_ge(lr_act, lbase + 2)
                        fn(lnst[:, 4, :], lnst[:, 3, :], ACT.Square).then_inc(lr_act, 1)
                    if new:
                        act.wait_ge(rs_act, rbase + 1)
                        if t >= 1:
                            act.wait_ge(outs_done, b * NSB + n)
                        fn(r0[:, :, :], lnn[:, :, :], ACT.Exp, scale=-0.5, bias=half_ln[0:NF2]).then_inc(rs_act, 1)
                        act.wait_ge(rs_act, rbase + 2)
                        fn(lnn[:, :, :], r0[:, :, :], ACT.Square).then_inc(rs_act, 1)

                bodies(act, layer1, NSB, 4, LBODY)

        @block.gpsimd
        def _(pool):
            tt = nc.gpsimd.tensor_tensor
            with pool.Fori(0, B) as b:
                def z_plus_y(m, s, g):
                    t = s - 3
                    if t >= 0:
                        pool.wait_ge(z_done, b * UNITS + m - 2)
                        tt(zring[:, t % 2, :], zring[:, t % 2, :], yring[:, t % 4, :],
                           ALU.add).then_inc(zs_done, 1)

                bodies(pool, z_plus_y, N0, 3, BODY)

                def apply(m, s, g):
                    if s % 2 == 1:
                        pool.wait_ge(saca_done, b * (UNITS // 2) + pair_of(m, s, g, BODY) + 1)
                        tt(unit(m), unit(m), pairs(saca[:, (s // 2) % 2, :]), ALU.mult).then_inc(out2_done[1], 1)

                bodies(pool, apply, N0, 0, BODY)

                def residual0(m, s, g):
                    if s % 2 == 1:
                        t = s % 16
                        if t % 4 == 1:
                            pool.wait_ge(xr_sems[(t // 4 + 1) % 4], b * 128 + g * 32 + 32)
                        pool.wait_ge(gs_done, b * UNITS + m + 1)
                        xs = xring[:, (t // 4 + 1) % 4, 512 * (t % 4):512 * (t % 4) + 512]
                        tt(xs, xs, gring[:, s % 4, :], ALU.add).then_inc(x1_done[1], 1)

                bodies(pool, residual0, N0, 0, 16, peel=16)

                pool.wait_ge(ln_ready, b + 1)

                def layer1(m, s, g):
                    n, t = m - 1, s - 1
                    if 3 <= s < NSB + 3:
                        pool.wait_ge(dsq_done, b * 3 * NSB + 3 * m - 6)
                        for j in range(3):
                            last = tt(dev[:, (s - 3) % 2, j], dev[:, (s - 3) % 2, j], hdw[:, (s - 3) % 4, :, 3 * E:E4], ALU.mult)
                        last.then_inc(vv_done, 1)
                    if 0 <= t < NSB:
                        pool.wait_ge(guard_done, b * NSB + n + 1)
                        if t >= 1:
                            pool.wait_ge(cross_done, b * NSB + n)
                        tt(prod[:, 0:2, :], gspec[:, 0:2, :], gspec[:, 2:4, :], ALU.mult)
                        tt(prod[:, 2, :], gspec[:, 1, :], gspec[:, 2, :], ALU.mult)
                        tt(prod[:, 3, :], gspec[:, 0, :], gspec[:, 3, :], ALU.mult).then_inc(sprod_done, 1)
                        pool.wait_ge(sprod_done, b * NSB + n + 1)
                        if t >= 2:
                            pool.wait_ge(outs_done, b * NSB + n - 1)
                        tt(cross[:, t % 2, 0, :], prod[:, 0, :], prod[:, 1, :], ALU.add)
                        tt(cross[:, t % 2, 1, :], prod[:, 2, :], prod[:, 3, :], ALU.subtract).then_inc(cross_done, 1)
                        pool.wait_ge(sq_done, b * NSB + n + 1)
                        if t >= 1:
                            pool.wait_ge(mag_done, b * NSB + n)
                        sv = mask.rearrange("p (a c) n -> p a c n", c=2)
                        tt(n2[:, :, :], sv[:, :, 0, :], sv[:, :, 1, :], ALU.add).then_inc(n2_done, 1)
                    if s < NSB:
                        k = s % 2
                        pool.wait_ge(ft_done, b * USES + use(m, s, 3) + 1)
                        tt(pprod[:, 0:2, :], spec[:, k, 0:2, :], spec[:, k, 2:4, :], ALU.mult)
                        tt(pprod[:, 2, :], spec[:, k, 0, :], spec[:, k, 3, :], ALU.mult)
                        tt(pprod[:, 3, :], spec[:, k, 1, :], spec[:, k, 2, :], ALU.mult).then_inc(qkp_done, 1)
                        pool.wait_ge(ft_done, b * USES + use(m, s, 5) + 1)
                        v = spec[:, k, 6:8, :].rearrange("p a (b e) -> p (a b) e", e=E)
                        tt(v, v, param[:, :].unsqueeze(1).to_broadcast([NF2, 2 * BLK, E]),
                           ALU.mult).then_inc(vpar_done, 1)
                        pool.wait_ge(qkp_done, b * NSB + m + 1)
                        tt(spec[:, k, 4, :], pprod[:, 0, :], pprod[:, 1, :], ALU.subtract)
                        tt(spec[:, k, 5, :], pprod[:, 2, :], pprod[:, 3, :], ALU.add).then_inc(qk_done, 1)

                bodies(pool, layer1, NSB, 3, LBODY)

        @block.vector
        def _(dve):
            v = nc.vector
            v.memset(caw1[:, :], 0.0)
            v.memset(W1[:, :], 0.0).then_inc(memset_done, 1)
            v.memset(half_ln, 5.545177444479562)
            v.memset(PW5[:, :], 0.0)
            v.memset(band7_new, 0.0)
            v.memset(ones_row[:, :], 1.0).then_inc(memset_done, 1)
            dve.wait_ge(memset_done, 2)
            dve.wait_ge(loaded, 16 * len(loads))
            steps = [0]

            def link(ins):
                steps[0] += 1
                ins.then_inc(v_setup, 1)
                dve.wait_ge(v_setup, steps[0])

            dve.wait_ge(p_setup, 8)
            link(v.tensor_tensor(cbias, psum[:, 0, 0:1], pwb, ALU.add))
            link(v.tensor_copy(saw[:, :], psum[:, 1, 0:99]))
            link(v.tensor_copy(sa_b, saw[:, 98:99]))
            for k in range(6):
                v.tensor_copy(wdb.rearrange("p t n -> p (t n)")[:, 456 * k:456 * k + 456], psum[:, 2 + k, 0:456])
            for tap in range(25):
                v.tensor_scalar(dense5[:, tap, :], pwT[:, 2, :], dwc[:, 10 + tap:11 + tap], None, ALU.mult)
            link(v.memset(padrow[:, :], 0.0))
            for tap in range(9):
                at = (tap // 3 + 1) * 5 + tap % 3 + 1
                v.scalar_tensor_tensor(dense5[:, at, :], pwT[:, 1, :], dwc[:, 1 + tap:2 + tap],
                                       dense5[:, at, :], ALU.mult, ALU.add)
            link(v.memset(padrow[:, :], 0.0))
            link(v.scalar_tensor_tensor(dense5[:, 12, :], pwT[:, 0, :], dwc[:, 0:1],
                                        dense5[:, 12, :], ALU.mult, ALU.add))
            for part, qi, e in ((0, 0, 0), (0, 1, 0), (1, 0, 1), (1, 1, -1)):
                for qo in range(2):
                    dy = 2 * e + qi - qo
                    v.tensor_copy(K5[64 * qi:64 * qi + 64, part, :, 64 * qo:64 * qo + 64],
                                  dense5[64 * qi:64 * qi + 64, 5 * (dy + 2):5 * (dy + 2) + 5, :])
            for q, row, other in ((0, 0, 3), (1, 4, 1)):
                v.tensor_copy(PW5[64 * q:64 * q + 64, 64 * q:64 * q + 64], pwT[64 * q:64 * q + 64, 2, :])
                half = slice(64 * q, 64 * q + 64)
                v.tensor_copy(tap_w[half, 0:5], dwc[half, 10 + 5 * row:15 + 5 * row])
                for k, dx in enumerate((0, 4)):
                    v.tensor_copy(tap_w[half, 5 + k:6 + k], dwc[half, 20 + dx:21 + dx])
                    v.tensor_copy(tap_w[half, 7 + k:8 + k], dwc[half, 10 + 5 * other + dx:11 + 5 * other + dx])
            for dx in range(7):
                for n in range(14):
                    ins = v.scalar_tensor_tensor(band7_new[:, n, :], bands[:, dx:dx + BAND_N],
                                                 saw[:, 7 * n + dx:7 * n + dx + 1], band7_new[:, n, :],
                                                 ALU.mult, ALU.add)
                link(ins)
            for dx in range(3):
                for q in range(2):
                    v.tensor_tensor(WA[64 * q:64 * q + 64, dx, :], whT[64 * q:64 * q + 64],
                                    wdb[64 * q:64 * q + 64, 3 * q + dx, :], ALU.mult)
            for q in range(2):
                v.tensor_tensor(WB[64 * q:64 * q + 64, 0, :], whT[64 * q:64 * q + 64],
                                wdb[64 * q:64 * q + 64, 6 + q, :], ALU.mult)
            v.tensor_tensor(WB[0:64, 1, :], whT[0:64], wdb[0:64, 8, :], ALU.mult)
            for j in range(3):
                v.tensor_scalar(wp4[:, j, :], wpr[:, j, :], lnw[:, j:j + 1], None, ALU.mult)
            link(v.tensor_scalar(wp4[:, 3, :], wpr[:, 0, :], lnb[:, 0:1], None, ALU.mult))
            for j in (1, 2):
                link(v.scalar_tensor_tensor(wp4[:, 3, :], wpr[:, j, :], lnb[:, j:j + 1], wp4[:, 3, :],
                                            ALU.mult, ALU.add))
            v.memset(padrow[:, :], 0.0).then_inc(wp4_done, 1)
            dve.wait_ge(wp4_done, 1)
            v.memset(padrow[:, :], 0.0).then_inc(setup_done, 1)

            with dve.Fori(0, B) as b:
                dve.wait_ge(image_done, b + 1)
                at = [0]

                def small(ins):
                    at[0] += 1
                    ins.then_inc(gn, 1)
                    dve.wait_ge(gn, b * G_V + at[0])

                def group_norm(st, mm0, acts):
                    v.memset(cols[:, 45:46], 0.0)
                    small(v.bn_aggr(cols[:, 16:18], st))
                    dve.wait_ge(gmm, b * G_M + mm0 + 1)
                    small(v.tensor_copy(cols[:, 18:19], psum[:, 7, 0:1]))
                    small(v.tensor_tensor(cols[:, 19:20], cols[:, 16:17], cols[:, 18:19], ALU.subtract))
                    small(v.scalar_tensor_tensor(cols[:, 20:21], cols[:, 19:20], cols[:, 19:20],
                                                 cols[:, 17:18], ALU.mult, ALU.add))
                    dve.wait_ge(gmm, b * G_M + mm0 + 2)
                    small(v.tensor_scalar(cols[:, 21:22], psum[:, 7, 0:1], GN_EPS, None, ALU.add))
                    dve.wait_ge(gact, b * G_A + acts)
                    small(v.reciprocal(cols[:, 23:24], cols[:, 22:23]))

                for ring in (hring, near, far, swap):
                    v.memset(ring[:, :, 0:2], 0.0)
                    v.memset(ring[:, :, 258:260], 0.0)
                v.memset(near[64:128, 1, 2:2 + W], 0.0)
                v.memset(far[0:64, 0, 2:2 + W], 0.0)
                with dve.Fori(0, N_CHUNKS // 4) as i:
                    for k in range(4):
                        dve.wait_ge(x_in_sems[k], b * 128 + i * 32 + 32)
                        for u in range(4):
                            t = i * 16 + (4 * k + u)
                            v.bn_stats(stats[:, bass.ds(t, 1), :],
                                       img[:, bass.ds(t * 2, 2), :]).then_inc(stat_done, 1)
                dve.wait_ge(stat_done, b * UNITS + UNITS)
                group_norm(stats[:, :, :], 0, 1)

                mean, rstd, ca = cols[:, 18:19], cols[:, 23:24], cols[:, 31:32]

                def mix(m, s, g):
                    if s < N0:
                        if s >= 4:
                            dve.wait_ge(c1_done, b * UNITS + m - 3)
                            dve.wait_ge(zs_done, b * UNITS + m - 3)
                        v.tensor_scalar(pairs(yring[:, s % 4, :]), unit(m), mean, rstd,
                                        ALU.subtract, ALU.mult).then_inc(y_done, 1)
                    if s == N0:
                        dve.wait_ge(c5_done, b * UNITS + N0 - 4)
                        dve.wait_ge(taps_done, b * TAPS * UNITS + TAPS * (N0 - 4))
                        v.memset(near[0:64, RP % HR, 2:2 + W], 0.0)
                        v.memset(far[64:128, (RP - 1) % HR, 2:2 + W], 0.0).then_inc(edge_done, 1)
                        dve.wait_ge(edge_done, b + 1)
                    if 2 <= s < N0 + 2:
                        t = s - 2
                        dve.wait_ge(h_done, b * UNITS + (m if t < N0 - 1 else m - 1))
                        if t >= 2:
                            dve.wait_ge(c5_done, b * UNITS + m - 3)
                        o = tapsum[:, t % 2, :].rearrange("p (r w) -> p r w", w=W)
                        at = (2 * t) % HR
                        taps = ([(far, dx) for dx in range(5)] + [(hring, dx) for dx in (0, 4)]
                                + [(swap, dx) for dx in (0, 4)])
                        for k, (ring, dx) in enumerate(taps):
                            rows = ring[:, at:at + 2, dx:dx + W]
                            if k == 0:
                                i = v.tensor_scalar(o, rows, tap_w[:, 0:1], None, ALU.mult)
                            else:
                                dve.wait_ge(taps_done, b * TAPS * UNITS + TAPS * m - 2 * TAPS + k)
                                i = v.scalar_tensor_tensor(o, rows, tap_w[:, k:k + 1], o, ALU.mult, ALU.add)
                            i.then_inc(taps_done, 1)
                    if s >= 5:
                        dve.wait_ge(img_done, b * UNITS + m - 4)
                        v.tensor_reduce(mxs[:, bass.ds(m - 5, 1)], unit(m - 5), AX.XY, ALU.max)
                        v.tensor_reduce(sms[:, bass.ds(m - 5, 1)], unit(m - 5), AX.XY,
                                        ALU.add).then_inc(red_done, 1)

                bodies(dve, mix, N0, 5, BODY)
                dve.wait_ge(red_done, b * UNITS + UNITS)
                small(v.tensor_reduce(cols[:, 24:25], sms[:, :], AX.X, ALU.add))
                small(v.tensor_reduce(cols[:, 25:26], mxs[:, :], AX.X, ALU.max))
                dve.wait_ge(gmm, b * G_M + 3)
                small(v.tensor_copy(cols[:, 26:27], psum[:, 7, 0:1]))
                dve.wait_ge(gmm, b * G_M + 4)
                small(v.tensor_tensor(cols[:, 27:28], psum[:, 7, 0:1], cols[:, 25:26], ALU.max))
                dve.wait_ge(gmm, b * G_M + 6)
                small(v.tensor_reduce(cols[:, 30:31], psum[:, 7, 0:2], AX.X, ALU.add))

                v.memset(maps[:, :, :, 0:3], 0.0)
                v.memset(maps[:, :, :, H + 3:H + 6], 0.0)

                def reduce_maps(m, s, g):
                    dve.wait_ge(tr_done, b * UNITS + m + 1)
                    for r in range(2):
                        o = psum[:, 2 * (s % 2) + r, 0:260].rearrange("p (h n) -> p h n", h=2)
                        rows = bass.ds(m * 4 + (2 * r + 3), 2)
                        v.tensor_reduce(maps[:, 1, :, rows], o[:, :, 0:128].rearrange("p h (q c) -> p h q c", q=2),
                                        AX.X, ALU.max)
                        last = v.tensor_copy(maps[:, 0, :, rows], o[:, :, 128:130])
                    last.then_inc(map_done, 1)

                bodies(dve, reduce_maps, N0, 0, BODY)

                dve.wait_ge(gact, b * G_A + 3)

                def apply(m, s, g):
                    half = b * (UNITS // 2) + pair_of(m, s, g, BODY)
                    if s < N0 and s % 2 == 0:
                        dve.wait_ge(sab_done, b * UNITS + m + 1)
                        v.scalar_tensor_tensor(unit(m), unit(m), ca, pairs(bank(s % 4)),
                                               ALU.mult, ALU.mult).then_inc(out2_done[0], 1)
                    if s >= 1:
                        dve.wait_ge(out2_done[(s - 1) % 2], half + s % 2)
                        v.bn_stats(stats[:, bass.ds(m - 1, 1), :], unit(m - 1)).then_inc(st2_done, 1)

                bodies(dve, apply, N0, 1, BODY)
                dve.wait_ge(st2_done, b * UNITS + UNITS)
                group_norm(stats[:, :, :], 6, 4)
                small(v.tensor_tensor(cols[:, 32:33], cols[:, 23:24], gn_g, ALU.mult))
                small(v.tensor_tensor(cols[:, 33:34], cols[:, 18:19], cols[:, 32:33], ALU.mult))
                small(v.tensor_tensor(cols[:, 34:35], gn_b, cols[:, 33:34], ALU.subtract))

                def x_unit(s):
                    t = s % 16
                    return xring[:, (t // 4 + 1) % 4, 512 * (t % 4):512 * (t % 4) + 512]

                def residual0(m, s, g):
                    half = b * (UNITS // 2) + pair_of(m, s, g, 16)
                    if s < N0 and s % 2 == 0:
                        if s % 4 == 0:
                            dve.wait_ge(xr_sems[(s // 4 + 1) % 4], b * 128 + g * 32 + 32)
                        dve.wait_ge(gs_done, b * UNITS + m + 1)
                        v.tensor_tensor(x_unit(s), x_unit(s), gring[:, s % 4, :], ALU.add).then_inc(x1_done[0], 1)
                    if s >= 1:
                        dve.wait_ge(x1_done[(s - 1) % 2], half + s % 2)
                        v.bn_stats(stats[:, bass.ds(m - 1, 1), :], x_unit(s - 1)).then_inc(st3_done, 1)

                bodies(dve, residual0, N0, 1, 16, peel=16)
                dve.wait_ge(st3_done, b * UNITS + UNITS)
                group_norm(stats[:, :, :], 8, 5)
                v.tensor_copy(padrow[:, :], mean[0:64].to_broadcast([64, W])).then_inc(pad_done, 1)
                for k in range(2):
                    v.memset(ynorm[:, k, 0, 0:1, :], 0.0)
                    v.memset(ynorm[:, k, 0, W + 1:W + 2, :], 0.0)
                    v.memset(ynorm[0:64, k, 1, 0:1, :], 0.0)
                    v.memset(ynorm[0:64, k, 1, W + 1:W + 2, :], 0.0)
                    last = v.memset(ynorm[64:128, k, 1, W:W + 2, :], 0.0)
                last.then_inc(ln_ready, 1)

                def guard(n, t):
                    k = t % 2
                    dve.wait_ge(abs_done, b * NSB + n + 1)
                    v.tensor_scalar(mask, mask, THR, BIG, ALU.is_ge, ALU.mult).then_inc(mask_done, 1)
                    dve.wait_ge(mask_done, b * NSB + n + 1)
                    if t >= 1:
                        dve.wait_ge(sprod_done, b * NSB + n)
                    if t >= 2:
                        dve.wait_ge(outs_done, b * NSB + n - 1)
                    flat = "p a n -> p (a n)"
                    v.scalar_tensor_tensor(gspec.rearrange(flat), mask[:, 0:6, :].rearrange(flat), THR,
                                           spec[:, k, 0:6, :].rearrange(flat), ALU.add, ALU.max)
                    v.scalar_tensor_tensor(gv[:, k].rearrange(flat), mask[:, 6:8, :].rearrange(flat), THR,
                                           spec[:, k, 6:8, :].rearrange(flat), ALU.add, ALU.max).then_inc(guard_done, 1)

                def newton(n, t):
                    dve.wait_ge(rs_act, b * 3 * NSB + 3 * n + 3)
                    v.scalar_tensor_tensor(lnn[:, :, :], lnn[:, :, :], -0.5, n2[:, :, :],
                                           ALU.mult, ALU.mult).then_inc(rs_dve, 1)
                    dve.wait_ge(rs_dve, b * 2 * NSB + 2 * n + 1)
                    v.scalar_tensor_tensor(roots, lnn[:, :, :], 1.5, r0[:, :, :],
                                           ALU.add, ALU.mult).then_inc(rs_dve, 1)
                    dve.wait_ge(rs_dve, b * 2 * NSB + 2 * n + 2)
                    v.tensor_tensor(mags[:, 0:2, :], n2[:, 2:4, :], roots[:, 2:4, :], ALU.mult)
                    v.tensor_tensor(mags[:, 2, :], roots[:, 0, :], roots[:, 1, :], ALU.mult).then_inc(mag_done, 1)

                def amplitudes(n, t):
                    dve.wait_ge(mag_done, b * NSB + n + 1)
                    v.tensor_tensor(amps[:, 0:2, :], mags[:, 0:2, :],
                                    mags[:, 2, :].unsqueeze(1).to_broadcast([NF2, 2, SBN]), ALU.mult)
                    v.tensor_tensor(amps[:, 2, :], mags[:, 0, :], roots[:, 3, :], ALU.mult).then_inc(amp_done, 1)

                def spectra(n, t):
                    dve.wait_ge(amp_done, b * NSB + n + 1)
                    dve.wait_ge(cross_done, b * NSB + n + 1)
                    if t >= 1:
                        dve.wait_ge(idft_done, b * 3 * NSB + 3 * n)
                    for j, (amp, z) in enumerate(((1, cross[:, t % 2]), (2, gv[:, t % 2]), (0, cross[:, t % 2]))):
                        last = v.tensor_tensor(outs[:, 2 * j:2 * j + 2, :], z[:, 0:2, :],
                                               amps[:, amp, :].unsqueeze(1).to_broadcast([NF2, 2, SBN]), ALU.mult)
                    last.then_inc(outs_done, 1)

                def deviations(n, t):
                    if t >= 2:
                        dve.wait_ge(cat_done, b * NSB + n - 1)
                    for j in range(3):
                        dve.wait_ge(idft_done, b * 3 * NSB + 3 * n + (j + 1))
                        o = psum[:, 5 + j, 0:SBN].rearrange("p (b e) -> p b e", e=E)
                        v.tensor_reduce(lnst[:, 6, 4 * j:4 * j + 4], o, AX.X, ALU.add).then_inc(sum_done, 1)
                        dve.wait_ge(sum_done, b * 3 * NSB + 3 * n + (j + 1))
                        v.scalar_tensor_tensor(dev[:, t % 2, j], bc(lnst[:, 6, 4 * j:4 * j + 4], E), -1.0 / E, o,
                                               ALU.mult, ALU.add).then_inc(dev_done, 1)

                def variances(n, t):
                    dve.wait_ge(dsq_done, b * 3 * NSB + 3 * n + 3)
                    v.tensor_reduce(lnst[:, 0, :], devsq.rearrange("p j b e -> p (j b) e"), AX.X,
                                    ALU.add).then_inc(var_done, 1)
                    dve.wait_ge(var_done, b * 2 * NSB + 2 * n + 1)
                    v.tensor_scalar(lnst[:, 1, :], lnst[:, 0, :], 1.0 / E, 1e-5, ALU.mult,
                                    ALU.add).then_inc(var_done, 1)

                def normalised(n, t):
                    dve.wait_ge(lr_act, b * 3 * NSB + 3 * n + 3)
                    v.scalar_tensor_tensor(lnst[:, 5, :], lnst[:, 4, :], -0.5, lnst[:, 1, :],
                                           ALU.mult, ALU.mult).then_inc(lr_dve, 1)
                    dve.wait_ge(lr_dve, b * 2 * NSB + 2 * n + 1)
                    v.scalar_tensor_tensor(lnst[:, 7, :], lnst[:, 5, :], 1.5, lnst[:, 3, :],
                                           ALU.add, ALU.mult).then_inc(lr_dve, 1)
                    dve.wait_ge(lr_dve, b * 2 * NSB + 2 * n + 2)
                    dve.wait_ge(vv_done, b * NSB + n + 1)
                    if t >= 2:
                        dve.wait_ge(proj_done, b * NSB + n - 1)
                    for j in range(3):
                        last = v.tensor_tensor(cat[:, t % 2, :, E * j:E * j + E], dev[:, t % 2, j],
                                               bc(lnst[:, 7, 4 * j:4 * j + 4], E), ALU.mult)
                    last.then_inc(cat_done, 1)

                def residual1(n, t, loads_):
                    k = (t // SBROW) % 2
                    if t % SBROW == 0:
                        dve.wait_ge(os_sems[k], b * 256 + loads_ * 16)
                    dve.wait_ge(proj_done, b * NSB + n + 1)
                    c0 = 64 * (t % SBROW)
                    o = ostage[k][:, :, c0:c0 + 64]
                    v.tensor_tensor(o, o, psum[0:64, 2, :].rearrange("p (w r) -> p r w", r=P),
                                    ALU.add).then_inc(res_done, 1)

                def normalise_rows(row, k, part):
                    if part == 0:
                        dve.wait_ge(xp_done, b * 64 * PROWS + row * 64 + 64)
                        if not isinstance(row, int) or row >= 2:
                            dve.wait_ge(conv_done, b * 4 * NSB + row * 16 - 16)
                    p0, p1, a, w0 = ((0, 128, 0, 1), (0, 64, 1, 1), (64, 128, 1, 0))[part]
                    i = v.tensor_scalar(ynorm[p0:p1, k, a, w0:w0 + W, :].rearrange("p w r -> p r w"),
                                        xraw[p0:p1, a], mean[p0:p1], rstd[p0:p1], ALU.subtract, ALU.mult)
                    if part == 2:
                        i.then_inc(yp_done, 1)

                def layer1(m, s, g):
                    if s == 0:
                        for part in range(3):
                            normalise_rows(0, 0, part)
                    if s % SBROW >= 1 and s < NSB - SBROW:
                        row = m // SBROW if isinstance(m, int) else g * 2 + (s % LBODY) // SBROW
                        normalise_rows(row + 1, (s // SBROW + 1) % 2, s % SBROW - 1)
                    if s >= 5:
                        residual1(m - 5, s - 5, (m - 5) // 8 + 1 if isinstance(m, int) else g + (s % LBODY >= 5))
                    if 3 <= s < NSB + 3:
                        deviations(m - 3, s - 3)
                    if 4 <= s < NSB + 4:
                        normalised(m - 4, s - 4)
                    if 1 <= s < NSB + 1:
                        guard(m - 1, s - 1)
                    if 2 <= s < NSB + 2:
                        newton(m - 2, s - 2)
                    if 3 <= s < NSB + 3:
                        variances(m - 3, s - 3)
                    if 2 <= s < NSB + 2:
                        amplitudes(m - 2, s - 2)
                        spectra(m - 2, s - 2)

                bodies(dve, layer1, NSB, 5, LBODY, LBODY)


def constants():
    import numpy as np
    f = np.float32
    p = np.arange(128)
    q, c = p // 64, p % 64
    diag = np.zeros((128, 130), f)
    diag[p, p] = 1
    diag[p, 128 + q] = 1 / 64
    avg2 = (c[:, None] // 2 == c[None] // 2).astype(f) / 4
    avg8 = (c[:, None] // 8 == c[None] // 8).astype(f) / 16
    avgq = (c[:, None] == c[None]).astype(f) / (H * W)
    swapq = ((p[:, None] + 64) % 128 == p[None]).astype(f)
    bands = np.zeros((128, 198), f)
    bands[p, p + K0 - BAND_LO] = 1
    r, col = p % P, p // P
    patch, cc = col // 8, col % 8
    ky, kx = np.arange(NF) // 5, np.arange(NF) % 5
    theta = 2 * np.pi * (r[:, None] * ky[None] + cc[:, None] * kx[None]) / P
    FR, FI = np.zeros((128, NF2)), np.zeros((128, NF2))
    GR, GI = np.zeros((NF2, 128)), np.zeros((NF2, 128))
    weight = np.where((kx == 0) | (kx == 4), 1.0, 2.0) / (P * P)
    for a in range(2):
        own = (patch == a)[:, None]
        FR[:, NF * a:NF * a + NF] = own * np.cos(theta)
        FI[:, NF * a:NF * a + NF] = own * -np.sin(theta)
        GR[NF * a:NF * a + NF] = (own * np.cos(theta) * weight).T
        GI[NF * a:NF * a + NF] = (own * -np.sin(theta) * weight).T
    return dict(consts=np.concatenate([diag, avg2, avg8, avgq, swapq], 1), bands=bands,
                FR=FR.astype(f), FI=FI.astype(f), GR=GR.astype(f), GI=GI.astype(f))


def kernel(**inputs):
    import numpy as np
    import concourse.bacc as bacc
    from concourse.bass_utils import run_bass_kernel_spmd as run

    g = {k: np.asarray(a) for k, a in inputs.items()}
    L0, L1 = "L0_conv_", "L1_conv_"
    col = lambda a: a.reshape(-1, 1)
    laid = dict(
        x=g["x"],
        w1T=g[L0 + "conv1_w"][:, :, 0, 0].T, conv1_b=col(g[L0 + "conv1_b"]),
        gn_g=col(g[L0 + "gn_g"]), gn_b=col(g[L0 + "gn_b"]), pw_b=col(g[L0 + "pw_b"]),
        pwT=g[L0 + "pw_w"].reshape(C, 3, C).transpose(2, 1, 0).reshape(C, 3 * C),
        dwc=np.concatenate([g[L0 + f"dw{k}_w"].reshape(C, -1) for k in (1, 2, 3)], 1),
        dbc=np.stack([g[L0 + f"dw{k}_b"] for k in (1, 2, 3)], 1),
        caw1T=g[L0 + "ca_w1"].reshape(8, C).T, caw2T=g[L0 + "ca_w2"].reshape(C, 8).T,
        sarow=np.concatenate([g[L0 + "sa_w"].reshape(1, 98), g[L0 + "sa_b"].reshape(1, 1)], 1),
        wdrow=g[L1 + "w_dw"].reshape(E4, 9).T.reshape(1, 9 * E4),
        whT=g[L1 + "w_hidden"].T,
        param=g[L1 + "fft_param"].reshape(E, NF).T,
        wpT=g[L1 + "w_proj"].reshape(C, 3, E).transpose(2, 1, 0).reshape(E, 3 * C),
        lnw=np.stack([g[L1 + f"ln{k}_w"] for k in (1, 2, 3)], 1),
        lnb=np.stack([g[L1 + f"ln{k}_b"] for k in (1, 2, 3)], 1),
        **constants(),
    )
    B = g["x"].shape[0]
    nc = bacc.Bacc("TRN2", target_bir_lowering=False, num_devices=1)
    arrays, io = {}, {}
    for name, a in laid.items():
        a = np.ascontiguousarray(a)
        arrays[f"in_{name}"] = a
        io[name] = nc.dram_tensor(f"in_{name}", a.shape, mybir.dt.from_np(a.dtype), kind="ExternalInput").ap()
    out = nc.dram_tensor("out_0", (B, C, H, W), F32, kind="ExternalOutput").ap()
    build(nc, B, io, out)
    r = run(nc, [arrays], core_ids=[0])
    return r.results[0]["out_0"]
```
